# Optimizing a Trainium2 kernel written in Bass

```python
import numpy as np
import jax
import jax.numpy as jnp

def _softmax(x, axis=-1):
    return jax.nn.softmax(x, axis=axis)

def _gelu(x):
    return jax.nn.gelu(x, approximate=True)

def _silu(x):
    return jax.nn.silu(x)

def _sigmoid(x):
    return jax.nn.sigmoid(x)

def _layernorm(x, axis=-1, eps=1e-05):
    m = jnp.mean(x, axis=axis, keepdims=True)
    v = jnp.var(x, axis=axis, keepdims=True)
    return (x - m) / jnp.sqrt(v + eps)

def _scatter_add(tgt, idx, src, axis=0):
    return tgt.at[idx].add(src)

def _segment_sum(src, seg, n):
    return jax.ops.segment_sum(src, seg, n)
kernel_name = 'mk_perceiver_d2_seqx_r4_69144b'

def setup_inputs(seed: int=0):
    np.random.seed(seed)
    _w = jnp.asarray

    def _rec_inputs():
        import jax
        import jax.numpy as jnp
        _rk = jax.random.key(seed)
        x = -0.0002928 + 1 * jax.random.normal(jax.random.fold_in(_rk, 1), (32, 32, 256), jnp.float32)
        _lenS = 32 - jax.random.randint(jax.random.fold_in(_rk, 7), (32,), 0, max(1, 32 // 4) + 1, jnp.int32)
        _lenS2 = 257 - jax.random.randint(jax.random.fold_in(_rk, 8), (32,), 0, max(1, 257 // 4) + 1, jnp.int32)
        _ctx_1024P = jax.random.normal(jax.random.fold_in(_rk, 11), (32, 16, 256), jnp.float32)
        _ctx_1024c = jax.random.dirichlet(jax.random.fold_in(_rk, 511), 0.3 * jnp.ones((16,), jnp.float32), (32, 257))
        _ctx_1024t = jnp.einsum('bsk,bkd->bsd', _ctx_1024c, _ctx_1024P)
        _ctx_1024t = _ctx_1024t * jax.lax.rsqrt(jnp.mean(jnp.square(_ctx_1024t)) + 1e-12) * 0.953939
        ctx_1024 = -1.39393e-06 + 0.999914 * (_ctx_1024t + 0.3 * jax.random.normal(jax.random.fold_in(_rk, 611), (32, 257, 256), jnp.float32))
        return (x, ctx_1024)
    x, ctx_1024 = _rec_inputs()

    def _L0_xattn_setup():
        import jax, jax.numpy as jnp
        import numpy as np
        DIM_Q = 256
        DIM_KV = 256
        DIM_OUT = 256
        NUM_HEADS = 16
        HEAD_DIM = DIM_OUT // NUM_HEADS
        key = jax.random.key(seed)
        ks = jax.random.split(key, 11)
        B, NQ, NKV = (2, 512, 512)
        s_q = 1.0 / np.sqrt(DIM_Q)
        s_kv = 1.0 / np.sqrt(DIM_KV)
        s_o = 1.0 / np.sqrt(DIM_OUT)
        return {'query': jax.random.normal(ks[0], (B, NQ, DIM_Q), jnp.float32), 'key': jax.random.normal(ks[1], (B, NKV, DIM_KV), jnp.float32), 'value': jax.random.normal(ks[2], (B, NKV, DIM_KV), jnp.float32), 'Wq': jax.random.normal(ks[3], (DIM_Q, DIM_OUT), jnp.float32) * s_q, 'bq': jnp.zeros((DIM_OUT,), jnp.float32), 'Wk': jax.random.normal(ks[4], (DIM_KV, DIM_OUT), jnp.float32) * s_kv, 'bk': jnp.zeros((DIM_OUT,), jnp.float32), 'Wv': jax.random.normal(ks[5], (DIM_KV, DIM_OUT), jnp.float32) * s_kv, 'bv': jnp.zeros((DIM_OUT,), jnp.float32), 'Wo': jax.random.normal(ks[6], (DIM_OUT, DIM_OUT), jnp.float32) * s_o, 'bo': jnp.zeros((DIM_OUT,), jnp.float32)}
    _L0_xattn_all = _L0_xattn_setup()
    _L0_xattn_in = {k: v for k, v in _L0_xattn_all.items() if k in ('Wq', 'bq', 'Wk', 'bk', 'Wv', 'bv', 'Wo', 'bo')}
    del _L0_xattn_all

    def _L0_attn_setup():
        import jax, jax.numpy as jnp
        import numpy as np
        D_MODEL = 256
        N_HEADS = 16
        HEAD_DIM = D_MODEL // N_HEADS
        WINDOW = 128
        LOCAL_BLOCK = 64
        LATENT_TOKENS = 64
        LATENT_D = 64
        LATENT_HEADS = 4
        LATENT_HD = LATENT_D // LATENT_HEADS
        NEG = -1000000000.0

        def _local_attention(q, k, v):
            B, H, S, hd = q.shape
            bs = min(S, max(WINDOW, LOCAL_BLOCK))
            nb = S // bs
            w = WINDOW
            L = bs + w - 1
            k_pad = jnp.pad(k, ((0, 0), (0, 0), (w - 1, 0), (0, 0)))
            v_pad = jnp.pad(v, ((0, 0), (0, 0), (w - 1, 0), (0, 0)))
            starts = jnp.arange(nb) * bs
            idx = starts[:, None] + jnp.arange(L)[None, :]
            kb = k_pad[:, :, idx]
            vb = v_pad[:, :, idx]
            qb = q.reshape(B, H, nb, bs, hd)
            q_pos = starts[:, None] + jnp.arange(bs)[None, :]
            k_gpos = starts[:, None] + jnp.arange(L)[None, :] - (w - 1)
            dist = q_pos[:, :, None] - k_gpos[:, None, :]
            allowed = (dist > 0) & (dist <= w) & (k_gpos[:, None, :] >= 0)
            scale = 1.0 / np.sqrt(hd)
            scores = jnp.einsum('bhnqd,bhnkd->bhnqk', qb, kb) * scale
            scores = jnp.where(allowed, scores, NEG)
            attn = jax.nn.softmax(scores, axis=-1)
            attn = jnp.where(allowed.any(-1)[None, None, :, :, None], attn, 0.0)
            out = jnp.einsum('bhnqk,bhnkd->bhnqd', attn, vb)
            return out.reshape(B, H, S, hd)
        key = jax.random.key(seed)
        ks = jax.random.split(key, 14)
        B, S = (2, 1024)
        s = 0.02
        f32 = jnp.float32
        return {'x': jax.random.normal(ks[0], (B, S, D_MODEL), f32), 'qkv_w': jax.random.normal(ks[1], (D_MODEL, 3 * D_MODEL), f32) * s, 'qkv_b': jnp.zeros((3 * D_MODEL,), f32), 'rq_w': jax.random.normal(ks[2], (D_MODEL, LATENT_D), f32) * s, 'rq_b': jnp.zeros((LATENT_D,), f32), 'rkv_w': jax.random.normal(ks[3], (D_MODEL, 2 * LATENT_D), f32) * s, 'rkv_b': jnp.zeros((2 * LATENT_D,), f32), 'rout_w': jax.random.normal(ks[4], (LATENT_D, D_MODEL), f32) * s, 'rout_b': jnp.zeros((D_MODEL,), f32), 'out_w': jax.random.normal(ks[5], (D_MODEL, D_MODEL), f32) * s, 'out_b': jnp.zeros((D_MODEL,), f32), 'gl_w': jax.random.normal(ks[6], (HEAD_DIM, 1), f32) * s, 'gr_w': jax.random.normal(ks[7], (HEAD_DIM, 1), f32) * s}
    _L0_attn_all = _L0_attn_setup()
    _L0_attn_in = {k: v for k, v in _L0_attn_all.items() if k in ('qkv_w', 'qkv_b', 'rq_w', 'rq_b', 'rkv_w', 'rkv_b', 'rout_w', 'rout_b', 'out_w', 'out_b', 'gl_w', 'gr_w')}
    del _L0_attn_all

    def _L0_ffn_setup():
        import jax, jax.numpy as jnp
        import numpy as np
        B, N, D, H, E = (4, 256, 256, 16, 8)
        DK = D // H
        HID = 4 * D
        EPS = 1e-05

        def _layernorm(x, w, b):
            m = jnp.mean(x, axis=-1, keepdims=True)
            v = jnp.mean(jnp.square(x - m), axis=-1, keepdims=True)
            return (x - m) * jax.lax.rsqrt(v + EPS) * w + b

        def _msa(x, w_qkv, w_proj):
            b, n, d = x.shape
            qkv = (x @ w_qkv).reshape(b, n, 3, H, DK)
            q = qkv[:, :, 0].transpose(0, 2, 1, 3)
            k = qkv[:, :, 1].transpose(0, 2, 1, 3)
            v = qkv[:, :, 2].transpose(0, 2, 1, 3)
            attn = jnp.einsum('bhnd,bhmd->bhnm', q, k) * (1.0 / np.sqrt(DK))
            attn = jax.nn.softmax(attn, axis=-1)
            y = jnp.einsum('bhnm,bhmd->bhnd', attn, v)
            y = y.transpose(0, 2, 1, 3).reshape(b, n, d)
            return y @ w_proj

        def _moe_mlp(x, gate_w, gate_b, w1, w2):
            b, n, d = x.shape
            xf = x.reshape(b * n, d)
            logits = xf @ gate_w + gate_b
            one_hot = jax.nn.one_hot(jnp.argmax(logits, axis=-1), E, dtype=xf.dtype)
            h = jax.nn.gelu(jnp.einsum('td,edh->teh', xf, w1), approximate=True)
            y = jnp.einsum('teh,ehd->ted', h, w2)
            out = jnp.einsum('te,ted->td', one_hot, y)
            return out.reshape(b, n, d)
        key = jax.random.key(seed)
        ks = jax.random.split(key, 8)
        s = 0.02
        return {'x': jax.random.normal(ks[0], (B, N, D), jnp.float32), 'ln1_w': jnp.ones((D,), jnp.float32), 'ln1_b': jnp.zeros((D,), jnp.float32), 'w_qkv': jax.random.normal(ks[1], (D, 3 * D), jnp.float32) * s, 'w_proj': jax.random.normal(ks[2], (D, D), jnp.float32) * s, 'ln2_w': jnp.ones((D,), jnp.float32), 'ln2_b': jnp.zeros((D,), jnp.float32), 'gate_w': jax.random.normal(ks[3], (D, E), jnp.float32) * s, 'gate_b': jnp.zeros((E,), jnp.float32), 'w1': jax.random.normal(ks[4], (E, D, HID), jnp.float32) * s, 'w2': jax.random.normal(ks[5], (E, HID, D), jnp.float32) * s}
    _L0_ffn_all = _L0_ffn_setup()
    _L0_ffn_in = {k: v for k, v in _L0_ffn_all.items() if k in ('ln1_w', 'ln1_b', 'w_qkv', 'w_proj', 'ln2_w', 'ln2_b', 'gate_w', 'gate_b', 'w1', 'w2')}
    del _L0_ffn_all

    def _L1_xattn_setup():
        import jax, jax.numpy as jnp
        import numpy as np
        DIM = 256
        NUM_HEADS = 16
        HEAD_DIM = DIM // NUM_HEADS
        key = jax.random.key(seed)
        ks = jax.random.split(key, 11)
        B, N, C = (2, 512, DIM)
        s = 1.0 / np.sqrt(C)
        inp = {'q': jax.random.normal(ks[0], (B, N, C), jnp.float32), 'k': jax.random.normal(ks[1], (B, N, C), jnp.float32), 'v': jax.random.normal(ks[2], (B, N, C), jnp.float32), 'Wq': jax.random.normal(ks[3], (C, C), jnp.float32) * s, 'bq': jnp.zeros((C,), jnp.float32), 'Wk': jax.random.normal(ks[4], (C, C), jnp.float32) * s, 'bk': jnp.zeros((C,), jnp.float32), 'Wv': jax.random.normal(ks[5], (C, C), jnp.float32) * s, 'bv': jnp.zeros((C,), jnp.float32), 'Wo': jax.random.normal(ks[6], (C, C), jnp.float32) * s, 'bo': jnp.zeros((C,), jnp.float32)}
        return inp
    _L1_xattn_all = _L1_xattn_setup()
    _L1_xattn_in = {k: v for k, v in _L1_xattn_all.items() if k in ('Wq', 'bq', 'Wk', 'bk', 'Wv', 'bv', 'Wo', 'bo')}
    del _L1_xattn_all

    def _L1_attn_setup():
        import jax, jax.numpy as jnp
        import numpy as np
        import math
        DIM = 256
        HEADS = 16
        DIM_HEAD = 64
        INNER = HEADS * DIM_HEAD
        NUM_BUCKETS = 32
        MAX_DISTANCE = 128

        def _relative_position_bucket(rel_pos, num_buckets=NUM_BUCKETS, max_distance=MAX_DISTANCE):
            n = -rel_pos
            num_buckets = num_buckets // 2
            ret = (n < 0).astype(jnp.int32) * num_buckets
            n = jnp.abs(n)
            max_exact = num_buckets // 2
            is_small = n < max_exact
            val_if_large = max_exact + (jnp.log(jnp.maximum(n, 1).astype(jnp.float32) / max_exact) / math.log(max_distance / max_exact) * (num_buckets - max_exact)).astype(jnp.int32)
            val_if_large = jnp.minimum(val_if_large, num_buckets - 1)
            return ret + jnp.where(is_small, n, val_if_large)

        def _rel_bias(rel_emb, n):
            pos = jnp.arange(n, dtype=jnp.int32)
            rel = pos[None, :] - pos[:, None]
            bucket = _relative_position_bucket(rel)
            vals = rel_emb[bucket]
            return jnp.transpose(vals, (2, 0, 1))
        key = jax.random.key(seed)
        ks = jax.random.split(key, 6)
        x = jax.random.normal(ks[0], (2, 512, DIM), dtype=jnp.float32)
        Wq = jax.random.normal(ks[1], (DIM, INNER), dtype=jnp.float32) * DIM ** (-0.5)
        Wkv = jax.random.normal(ks[2], (DIM, 2 * INNER), dtype=jnp.float32) * DIM ** (-0.5)
        Wo = jax.random.normal(ks[3], (INNER, DIM), dtype=jnp.float32) * INNER ** (-0.5)
        bo = jax.random.normal(ks[4], (DIM,), dtype=jnp.float32) * 0.01
        rel_emb = jax.random.normal(ks[5], (NUM_BUCKETS, HEADS), dtype=jnp.float32)
        return {'x': x, 'Wq': Wq, 'Wkv': Wkv, 'Wo': Wo, 'bo': bo, 'rel_emb': rel_emb}
    _L1_attn_all = _L1_attn_setup()
    _L1_attn_in = {k: v for k, v in _L1_attn_all.items() if k in ('Wq', 'Wkv', 'Wo', 'bo', 'rel_emb')}
    del _L1_attn_all

    def _L1_ffn_setup():
        import jax, jax.numpy as jnp
        import numpy as np
        S, B, H = (512, 2, 256)
        NUM_HEADS, NUM_KV_HEADS = (16, 4)
        HEAD_DIM = H // NUM_HEADS
        E, TOP_K, FFN = (16, 2, 512)
        CAP_FACTOR = 1.25
        EPS = 1e-05

        def _layernorm(x, w, b):
            mu = jnp.mean(x, axis=-1, keepdims=True)
            var = jnp.mean((x - mu) ** 2, axis=-1, keepdims=True)
            return (x - mu) * jax.lax.rsqrt(var + EPS) * w + b
        key = jax.random.key(seed)
        ks = jax.random.split(key, 6)
        qkv_out = (NUM_HEADS + 2 * NUM_KV_HEADS) * HEAD_DIM
        sdH = 1.0 / np.sqrt(H)
        sdF = 1.0 / np.sqrt(FFN)
        return {'hidden_states': jax.random.normal(ks[0], (S, B, H), jnp.float32), 'ln1_weight': jnp.ones((H,), jnp.float32), 'ln1_bias': jnp.zeros((H,), jnp.float32), 'ln2_weight': jnp.ones((H,), jnp.float32), 'ln2_bias': jnp.zeros((H,), jnp.float32), 'qkv_weight': jax.random.normal(ks[1], (qkv_out, H), jnp.float32) * sdH, 'proj_weight': jax.random.normal(ks[2], (H, H), jnp.float32) * sdH, 'router_weight': jax.random.normal(ks[3], (E, H), jnp.float32) * sdH, 'moe_w1': jax.random.normal(ks[4], (E, FFN, H), jnp.float32) * sdH, 'moe_w2': jax.random.normal(ks[5], (E, H, FFN), jnp.float32) * sdF}
    _L1_ffn_all = _L1_ffn_setup()
    _L1_ffn_in = {k: v for k, v in _L1_ffn_all.items() if k in ('ln1_weight', 'ln1_bias', 'ln2_weight', 'ln2_bias', 'qkv_weight', 'proj_weight', 'router_weight', 'moe_w1', 'moe_w2')}
    del _L1_ffn_all
    return {'x': x, 'ctx_1024': ctx_1024, 'L0_xattn_Wq': _L0_xattn_in['Wq'], 'L0_xattn_bq': _L0_xattn_in['bq'], 'L0_xattn_Wk': _L0_xattn_in['Wk'], 'L0_xattn_bk': _L0_xattn_in['bk'], 'L0_xattn_Wv': _L0_xattn_in['Wv'], 'L0_xattn_bv': _L0_xattn_in['bv'], 'L0_xattn_Wo': _L0_xattn_in['Wo'], 'L0_xattn_bo': _L0_xattn_in['bo'], 'L0_attn_qkv_w': _L0_attn_in['qkv_w'], 'L0_attn_qkv_b': _L0_attn_in['qkv_b'], 'L0_attn_rq_w': _L0_attn_in['rq_w'], 'L0_attn_rq_b': _L0_attn_in['rq_b'], 'L0_attn_rkv_w': _L0_attn_in['rkv_w'], 'L0_attn_rkv_b': _L0_attn_in['rkv_b'], 'L0_attn_rout_w': _L0_attn_in['rout_w'], 'L0_attn_rout_b': _L0_attn_in['rout_b'], 'L0_attn_out_w': _L0_attn_in['out_w'], 'L0_attn_out_b': _L0_attn_in['out_b'], 'L0_attn_gl_w': _L0_attn_in['gl_w'], 'L0_attn_gr_w': _L0_attn_in['gr_w'], 'L0_ffn_ln1_w': _L0_ffn_in['ln1_w'], 'L0_ffn_ln1_b': _L0_ffn_in['ln1_b'], 'L0_ffn_w_qkv': _L0_ffn_in['w_qkv'], 'L0_ffn_w_proj': _L0_ffn_in['w_proj'], 'L0_ffn_ln2_w': _L0_ffn_in['ln2_w'], 'L0_ffn_ln2_b': _L0_ffn_in['ln2_b'], 'L0_ffn_gate_w': _L0_ffn_in['gate_w'], 'L0_ffn_gate_b': _L0_ffn_in['gate_b'], 'L0_ffn_w1': _L0_ffn_in['w1'], 'L0_ffn_w2': _L0_ffn_in['w2'], 'L1_xattn_Wq': _L1_xattn_in['Wq'], 'L1_xattn_bq': _L1_xattn_in['bq'], 'L1_xattn_Wk': _L1_xattn_in['Wk'], 'L1_xattn_bk': _L1_xattn_in['bk'], 'L1_xattn_Wv': _L1_xattn_in['Wv'], 'L1_xattn_bv': _L1_xattn_in['bv'], 'L1_xattn_Wo': _L1_xattn_in['Wo'], 'L1_xattn_bo': _L1_xattn_in['bo'], 'L1_attn_Wq': _L1_attn_in['Wq'], 'L1_attn_Wkv': _L1_attn_in['Wkv'], 'L1_attn_Wo': _L1_attn_in['Wo'], 'L1_attn_bo': _L1_attn_in['bo'], 'L1_attn_rel_emb': _L1_attn_in['rel_emb'], 'L1_ffn_ln1_weight': _L1_ffn_in['ln1_weight'], 'L1_ffn_ln1_bias': _L1_ffn_in['ln1_bias'], 'L1_ffn_ln2_weight': _L1_ffn_in['ln2_weight'], 'L1_ffn_ln2_bias': _L1_ffn_in['ln2_bias'], 'L1_ffn_qkv_weight': _L1_ffn_in['qkv_weight'], 'L1_ffn_proj_weight': _L1_ffn_in['proj_weight'], 'L1_ffn_router_weight': _L1_ffn_in['router_weight'], 'L1_ffn_moe_w1': _L1_ffn_in['moe_w1'], 'L1_ffn_moe_w2': _L1_ffn_in['moe_w2']}

def reference(x, ctx_1024, L0_xattn_Wq, L0_xattn_bq, L0_xattn_Wk, L0_xattn_bk, L0_xattn_Wv, L0_xattn_bv, L0_xattn_Wo, L0_xattn_bo, L0_attn_qkv_w, L0_attn_qkv_b, L0_attn_rq_w, L0_attn_rq_b, L0_attn_rkv_w, L0_attn_rkv_b, L0_attn_rout_w, L0_attn_rout_b, L0_attn_out_w, L0_attn_out_b, L0_attn_gl_w, L0_attn_gr_w, L0_ffn_ln1_w, L0_ffn_ln1_b, L0_ffn_w_qkv, L0_ffn_w_proj, L0_ffn_ln2_w, L0_ffn_ln2_b, L0_ffn_gate_w, L0_ffn_gate_b, L0_ffn_w1, L0_ffn_w2, L1_xattn_Wq, L1_xattn_bq, L1_xattn_Wk, L1_xattn_bk, L1_xattn_Wv, L1_xattn_bv, L1_xattn_Wo, L1_xattn_bo, L1_attn_Wq, L1_attn_Wkv, L1_attn_Wo, L1_attn_bo, L1_attn_rel_emb, L1_ffn_ln1_weight, L1_ffn_ln1_bias, L1_ffn_ln2_weight, L1_ffn_ln2_bias, L1_ffn_qkv_weight, L1_ffn_proj_weight, L1_ffn_router_weight, L1_ffn_moe_w1, L1_ffn_moe_w2):
    import jax
    import jax.numpy as jnp

    def _L0_xattn_ref(query, key, value, Wq, bq, Wk, bk, Wv, bv, Wo, bo):
        import jax, jax.numpy as jnp
        import numpy as np
        DIM_Q = 256
        DIM_KV = 256
        DIM_OUT = 256
        NUM_HEADS = 16
        HEAD_DIM = DIM_OUT // NUM_HEADS
        B, NQ, _ = query.shape
        NKV = key.shape[1]
        Q = (query @ Wq + bq).reshape(B, NQ, NUM_HEADS, HEAD_DIM).transpose(0, 2, 1, 3)
        K = (key @ Wk + bk).reshape(B, NKV, NUM_HEADS, HEAD_DIM).transpose(0, 2, 1, 3)
        V = (value @ Wv + bv).reshape(B, NKV, NUM_HEADS, HEAD_DIM).transpose(0, 2, 1, 3)
        scores = jnp.einsum('bhqd,bhkd->bhqk', Q, K) / np.sqrt(HEAD_DIM).astype(np.float32)
        attn = jax.nn.softmax(scores, axis=-1)
        out = jnp.einsum('bhqk,bhkd->bhqd', attn, V)
        out = out.transpose(0, 2, 1, 3).reshape(B, NQ, DIM_OUT)
        return out @ Wo + bo

    def _L0_attn_ref(x, qkv_w, qkv_b, rq_w, rq_b, rkv_w, rkv_b, rout_w, rout_b, out_w, out_b, gl_w, gr_w):
        import jax, jax.numpy as jnp
        import numpy as np
        D_MODEL = 256
        N_HEADS = 16
        HEAD_DIM = D_MODEL // N_HEADS
        WINDOW = 128
        LOCAL_BLOCK = 64
        LATENT_TOKENS = 64
        LATENT_D = 64
        LATENT_HEADS = 4
        LATENT_HD = LATENT_D // LATENT_HEADS
        NEG = -1000000000.0

        def _local_attention(q, k, v):
            B, H, S, hd = q.shape
            bs = min(S, max(WINDOW, LOCAL_BLOCK))
            nb = S // bs
            w = WINDOW
            L = bs + w - 1
            k_pad = jnp.pad(k, ((0, 0), (0, 0), (w - 1, 0), (0, 0)))
            v_pad = jnp.pad(v, ((0, 0), (0, 0), (w - 1, 0), (0, 0)))
            starts = jnp.arange(nb) * bs
            idx = starts[:, None] + jnp.arange(L)[None, :]
            kb = k_pad[:, :, idx]
            vb = v_pad[:, :, idx]
            qb = q.reshape(B, H, nb, bs, hd)
            q_pos = starts[:, None] + jnp.arange(bs)[None, :]
            k_gpos = starts[:, None] + jnp.arange(L)[None, :] - (w - 1)
            dist = q_pos[:, :, None] - k_gpos[:, None, :]
            allowed = (dist > 0) & (dist <= w) & (k_gpos[:, None, :] >= 0)
            scale = 1.0 / np.sqrt(hd)
            scores = jnp.einsum('bhnqd,bhnkd->bhnqk', qb, kb) * scale
            scores = jnp.where(allowed, scores, NEG)
            attn = jax.nn.softmax(scores, axis=-1)
            attn = jnp.where(allowed.any(-1)[None, None, :, :, None], attn, 0.0)
            out = jnp.einsum('bhnqk,bhnkd->bhnqd', attn, vb)
            return out.reshape(B, H, S, hd)
        B, S, D = x.shape
        qkv = x @ qkv_w + qkv_b
        q, k, v = jnp.split(qkv, 3, axis=-1)

        def heads(t):
            return t.reshape(B, S, N_HEADS, HEAD_DIM).transpose(0, 2, 1, 3)
        local = _local_attention(heads(q), heads(k), heads(v))
        chunk = -(-S // min(LATENT_TOKENS, S))
        nlat = S // chunk
        pooled = x.reshape(B, nlat, chunk, D).mean(axis=2)
        chunk_ids = jnp.arange(S) // chunk
        rq = (x @ rq_w + rq_b).reshape(B, S, LATENT_HEADS, LATENT_HD).transpose(0, 2, 1, 3)
        rkv = pooled @ rkv_w + rkv_b
        rk, rv = jnp.split(rkv, 2, axis=-1)
        rk = rk.reshape(B, nlat, LATENT_HEADS, LATENT_HD).transpose(0, 2, 1, 3)
        rv = rv.reshape(B, nlat, LATENT_HEADS, LATENT_HD).transpose(0, 2, 1, 3)
        lscale = 1.0 / np.sqrt(LATENT_HD)
        lscores = jnp.einsum('bhsd,bhld->bhsl', rq, rk) * lscale
        lat_allowed = jnp.arange(nlat)[None, :] < chunk_ids[:, None]
        lscores = jnp.where(lat_allowed[None, None], lscores, NEG)
        lattn = jax.nn.softmax(lscores, axis=-1)
        lattn = jnp.where(lat_allowed.any(-1)[None, None, :, None], lattn, 0.0)
        lat_out = jnp.einsum('bhsl,bhld->bhsd', lattn, rv)
        lat_out = lat_out.transpose(0, 2, 1, 3).reshape(B, S, LATENT_D)
        remote = lat_out @ rout_w + rout_b
        remote_h = remote.reshape(B, S, N_HEADS, HEAD_DIM).transpose(0, 2, 1, 3)
        gate = jax.nn.sigmoid(local @ gl_w + remote_h @ gr_w)
        mixed = gate * local + (1.0 - gate) * remote_h
        mixed = mixed.transpose(0, 2, 1, 3).reshape(B, S, D)
        return mixed @ out_w + out_b

    def _L0_ffn_ref(x, ln1_w, ln1_b, w_qkv, w_proj, ln2_w, ln2_b, gate_w, gate_b, w1, w2):
        import jax, jax.numpy as jnp
        import numpy as np
        B, N, D, H, E = (4, 256, 256, 16, 8)
        DK = D // H
        HID = 4 * D
        EPS = 1e-05

        def _layernorm(x, w, b):
            m = jnp.mean(x, axis=-1, keepdims=True)
            v = jnp.mean(jnp.square(x - m), axis=-1, keepdims=True)
            return (x - m) * jax.lax.rsqrt(v + EPS) * w + b

        def _msa(x, w_qkv, w_proj):
            b, n, d = x.shape
            qkv = (x @ w_qkv).reshape(b, n, 3, H, DK)
            q = qkv[:, :, 0].transpose(0, 2, 1, 3)
            k = qkv[:, :, 1].transpose(0, 2, 1, 3)
            v = qkv[:, :, 2].transpose(0, 2, 1, 3)
            attn = jnp.einsum('bhnd,bhmd->bhnm', q, k) * (1.0 / np.sqrt(DK))
            attn = jax.nn.softmax(attn, axis=-1)
            y = jnp.einsum('bhnm,bhmd->bhnd', attn, v)
            y = y.transpose(0, 2, 1, 3).reshape(b, n, d)
            return y @ w_proj

        def _moe_mlp(x, gate_w, gate_b, w1, w2):
            b, n, d = x.shape
            xf = x.reshape(b * n, d)
            logits = xf @ gate_w + gate_b
            one_hot = jax.nn.one_hot(jnp.argmax(logits, axis=-1), E, dtype=xf.dtype)
            h = jax.nn.gelu(jnp.einsum('td,edh->teh', xf, w1), approximate=True)
            y = jnp.einsum('teh,ehd->ted', h, w2)
            out = jnp.einsum('te,ted->td', one_hot, y)
            return out.reshape(b, n, d)
        x = x + _msa(_layernorm(x, ln1_w, ln1_b), w_qkv, w_proj)
        x = x + _moe_mlp(_layernorm(x, ln2_w, ln2_b), gate_w, gate_b, w1, w2)
        return x

    def _L1_xattn_ref(q, k, v, Wq, bq, Wk, bk, Wv, bv, Wo, bo):
        import jax, jax.numpy as jnp
        import numpy as np
        DIM = 256
        NUM_HEADS = 16
        HEAD_DIM = DIM // NUM_HEADS
        B, Nq, C = q.shape
        Nkv = k.shape[1]
        H, D = (NUM_HEADS, HEAD_DIM)
        qh = (q @ Wq.T + bq).reshape(B, Nq, H, D).transpose(0, 2, 1, 3)
        kh = (k @ Wk.T + bk).reshape(B, Nkv, H, D).transpose(0, 2, 1, 3)
        vh = (v @ Wv.T + bv).reshape(B, Nkv, H, D).transpose(0, 2, 1, 3)
        scale = D ** (-0.5)
        attn = jax.nn.softmax(jnp.einsum('bhqd,bhkd->bhqk', qh, kh) * scale, axis=-1)
        out = jnp.einsum('bhqk,bhkd->bhqd', attn, vh)
        out = out.transpose(0, 2, 1, 3).reshape(B, Nq, C)
        return out @ Wo.T + bo

    def _L1_attn_ref(x, Wq, Wkv, Wo, bo, rel_emb):
        import jax, jax.numpy as jnp
        import numpy as np
        import math
        DIM = 256
        HEADS = 16
        DIM_HEAD = 64
        INNER = HEADS * DIM_HEAD
        NUM_BUCKETS = 32
        MAX_DISTANCE = 128

        def _relative_position_bucket(rel_pos, num_buckets=NUM_BUCKETS, max_distance=MAX_DISTANCE):
            n = -rel_pos
            num_buckets = num_buckets // 2
            ret = (n < 0).astype(jnp.int32) * num_buckets
            n = jnp.abs(n)
            max_exact = num_buckets // 2
            is_small = n < max_exact
            val_if_large = max_exact + (jnp.log(jnp.maximum(n, 1).astype(jnp.float32) / max_exact) / math.log(max_distance / max_exact) * (num_buckets - max_exact)).astype(jnp.int32)
            val_if_large = jnp.minimum(val_if_large, num_buckets - 1)
            return ret + jnp.where(is_small, n, val_if_large)

        def _rel_bias(rel_emb, n):
            pos = jnp.arange(n, dtype=jnp.int32)
            rel = pos[None, :] - pos[:, None]
            bucket = _relative_position_bucket(rel)
            vals = rel_emb[bucket]
            return jnp.transpose(vals, (2, 0, 1))
        b, n, _ = x.shape
        h, d = (HEADS, DIM_HEAD)
        scale = d ** (-0.5)
        q = (x @ Wq).reshape(b, n, h, d).transpose(0, 2, 1, 3)
        kv = x @ Wkv
        k, v = jnp.split(kv, 2, axis=-1)
        k = k.reshape(b, n, h, d).transpose(0, 2, 1, 3)
        v = v.reshape(b, n, h, d).transpose(0, 2, 1, 3)
        dots = jnp.einsum('bhid,bhjd->bhij', q, k) * scale
        dots = dots + _rel_bias(rel_emb, n)[None]
        attn = jax.nn.softmax(dots, axis=-1)
        out = jnp.einsum('bhij,bhjd->bhid', attn, v)
        out = out.transpose(0, 2, 1, 3).reshape(b, n, h * d)
        return out @ Wo + bo

    def _L1_ffn_ref(hidden_states, ln1_weight, ln1_bias, ln2_weight, ln2_bias, qkv_weight, proj_weight, router_weight, moe_w1, moe_w2):
        import jax, jax.numpy as jnp
        import numpy as np
        S, B, H = (512, 2, 256)
        NUM_HEADS, NUM_KV_HEADS = (16, 4)
        HEAD_DIM = H // NUM_HEADS
        E, TOP_K, FFN = (16, 2, 512)
        CAP_FACTOR = 1.25
        EPS = 1e-05

        def _layernorm(x, w, b):
            mu = jnp.mean(x, axis=-1, keepdims=True)
            var = jnp.mean((x - mu) ** 2, axis=-1, keepdims=True)
            return (x - mu) * jax.lax.rsqrt(var + EPS) * w + b
        S_, B_, H_ = hidden_states.shape
        dtype = hidden_states.dtype
        ln1 = _layernorm(hidden_states, ln1_weight, ln1_bias)
        qkv = jnp.einsum('sbh,oh->sbo', ln1, qkv_weight)
        q_sz = NUM_HEADS * HEAD_DIM
        kv_sz = NUM_KV_HEADS * HEAD_DIM
        q = qkv[..., :q_sz].reshape(S_, B_, NUM_HEADS, HEAD_DIM)
        k = qkv[..., q_sz:q_sz + kv_sz].reshape(S_, B_, NUM_KV_HEADS, HEAD_DIM)
        v = qkv[..., q_sz + kv_sz:].reshape(S_, B_, NUM_KV_HEADS, HEAD_DIM)
        rep = NUM_HEADS // NUM_KV_HEADS
        k = jnp.repeat(k, rep, axis=2)
        v = jnp.repeat(v, rep, axis=2)
        scale = 1.0 / np.sqrt(HEAD_DIM)
        scores = jnp.einsum('qbhd,kbhd->bhqk', q, k) * scale
        causal = jnp.tril(jnp.ones((S_, S_), bool))
        scores = jnp.where(causal, scores, jnp.asarray(-1e+30, dtype))
        attn = jax.nn.softmax(scores, axis=-1)
        attn_out = jnp.einsum('bhqk,kbhd->qbhd', attn, v).reshape(S_, B_, H_)
        proj_out = jnp.einsum('sbh,oh->sbo', attn_out, proj_weight)
        hidden_after_attn = hidden_states + proj_out
        ln2 = _layernorm(hidden_after_attn, ln2_weight, ln2_bias).reshape(-1, H_)
        T = ln2.shape[0]
        logits = ln2 @ router_weight.T
        probs = jax.nn.softmax(logits, axis=-1)
        top_p, top_i = jax.lax.top_k(probs, TOP_K)
        cap = int(np.ceil(T * TOP_K / E * CAP_FACTOR))
        exp_idx = top_i.reshape(-1)
        gate = top_p.reshape(-1).astype(dtype)
        tok = jnp.repeat(jnp.arange(T), TOP_K)
        onehot = jax.nn.one_hot(exp_idx, E, dtype=jnp.int32)
        pos = (jnp.cumsum(onehot, axis=0) * onehot).sum(-1) - 1
        keep = pos < cap
        pos_c = jnp.where(keep, pos, cap)
        buf = jnp.zeros((E, cap + 1, H_), dtype)
        buf = buf.at[exp_idx, pos_c].add(ln2[tok] * keep[:, None].astype(dtype))
        h1 = jax.nn.gelu(jnp.einsum('ech,efh->ecf', buf, moe_w1))
        h2 = jnp.einsum('ecf,ehf->ech', h1, moe_w2)
        out_ent = h2[exp_idx, pos_c] * (gate * keep.astype(dtype))[:, None]
        moe_out = jnp.zeros((T, H_), dtype).at[tok].add(out_ent)
        return hidden_after_attn + moe_out.reshape(S_, B_, H_)
    x = x + _L0_xattn_ref(_layernorm(x, axis=-1), ctx_1024, ctx_1024, L0_xattn_Wq, L0_xattn_bq, L0_xattn_Wk, L0_xattn_bk, L0_xattn_Wv, L0_xattn_bv, L0_xattn_Wo, L0_xattn_bo)
    x = x + _L0_attn_ref(_layernorm(x, axis=-1), L0_attn_qkv_w, L0_attn_qkv_b, L0_attn_rq_w, L0_attn_rq_b, L0_attn_rkv_w, L0_attn_rkv_b, L0_attn_rout_w, L0_attn_rout_b, L0_attn_out_w, L0_attn_out_b, L0_attn_gl_w, L0_attn_gr_w)
    x = x + _L0_ffn_ref(_layernorm(x, axis=-1), L0_ffn_ln1_w, L0_ffn_ln1_b, L0_ffn_w_qkv, L0_ffn_w_proj, L0_ffn_ln2_w, L0_ffn_ln2_b, L0_ffn_gate_w, L0_ffn_gate_b, L0_ffn_w1, L0_ffn_w2)
    x = x + _L1_xattn_ref(_layernorm(x, axis=-1), ctx_1024, ctx_1024, L1_xattn_Wq, L1_xattn_bq, L1_xattn_Wk, L1_xattn_bk, L1_xattn_Wv, L1_xattn_bv, L1_xattn_Wo, L1_xattn_bo)
    x = x + _L1_attn_ref(_layernorm(x, axis=-1), L1_attn_Wq, L1_attn_Wkv, L1_attn_Wo, L1_attn_bo, L1_attn_rel_emb)
    x = x + _L1_ffn_ref(_layernorm(x, axis=-1), L1_ffn_ln1_weight, L1_ffn_ln1_bias, L1_ffn_ln2_weight, L1_ffn_ln2_bias, L1_ffn_qkv_weight, L1_ffn_proj_weight, L1_ffn_router_weight, L1_ffn_moe_w1, L1_ffn_moe_w2)
    return x

_drawn_inputs = setup_inputs


def setup_inputs(seed=0):
    import zlib

    import numpy as np

    out = dict(_drawn_inputs(seed))
    spreads = {'L0_xattn_bq': (0.0, 0.322),
     'L0_xattn_bk': (0.0, 0.8),
     'L0_xattn_bv': (0.0, 0.1),
     'L0_xattn_bo': (0.0, 0.1),
     'L0_attn_qkv_b': (0.0, 0.483),
     'L0_attn_rq_b': (0.0, 0.8),
     'L0_attn_rkv_b': (0.0, 0.8),
     'L0_attn_rout_b': (0.0, 0.435),
     'L0_attn_out_b': (0.0, 0.1),
     'L0_ffn_ln1_w': (1.0, 0.6),
     'L0_ffn_ln1_b': (0.0, 0.8),
     'L0_ffn_ln2_w': (1.0, 0.2),
     'L0_ffn_ln2_b': (0.0, 0.388),
     'L0_ffn_gate_b': (0.0, 0.1),
     'L1_xattn_bq': (0.0, 0.646),
     'L1_xattn_bk': (0.0, 0.8),
     'L1_xattn_bv': (0.0, 0.1),
     'L1_xattn_bo': (0.0, 0.1),
     'L1_ffn_ln1_weight': (1.0, 0.2),
     'L1_ffn_ln1_bias': (0.0, 0.1),
     'L1_ffn_ln2_weight': (1.0, 0.592),
     'L1_ffn_ln2_bias': (0.0, 0.446)}
    factors = {'L0_attn_rq_w': 8.0,
     'L0_attn_rkv_w': 8.0,
     'L0_attn_rout_w': 7.546,
     'L0_attn_gl_w': 8.0,
     'L0_attn_gr_w': 8.0,
     'L1_attn_bo': 8.0}
    for name, (base, spread) in spreads.items():
        noise = np.random.default_rng([zlib.crc32(name.encode()), seed]).standard_normal(out[name].shape)
        drawn = base * np.exp(spread * noise) if base else spread * noise
        out[name] = jnp.asarray(drawn.astype(out[name].dtype))
    for name, factor in factors.items():
        out[name] = (out[name] * factor).astype(out[name].dtype)
    return out
```

```python
import concourse.bass as bass
from concourse import mybir
from contextlib import ExitStack

F32 = mybir.dt.float32
U32 = mybir.dt.uint32
I32 = mybir.dt.int32
ALU = mybir.AluOpType
ACT = mybir.ActivationFunctionType
AX = mybir.AxisListType

P = 128
D = 256
DK = D // P
SEQS, SEQ = 32, 32
TOK = SEQS * SEQ
TILES = TOK // P
SPT = P // SEQ
CTX = 257
HEADS = 16
HD = D // HEADS
HPG = 4
GROUPS = HEADS // HPG
EPS = 1e-5
MASKED = -1e30
LAT = 64

COLS = {}


def _column(name, n):
    COLS[name] = (sum(w for _, w in COLS.values()), n)


for _name, _n in (("L0x_bq", DK), ("L0x_bk", DK), ("L0x_bv", DK), ("L1x_bq", DK), ("L1x_bk", DK), ("L1x_bv", DK),
                  ("L0a_bk", DK), ("L0a_bv", DK), ("L0a_rout_b", DK), 
                  ("L0a_rkq_b", 1), ("L0a_rv_b", 1), ("L0a_gl", 1), ("L0a_gr", 1),
                  ("L0f_ln1_w", DK), ("L0f_ln1_b", DK), ("L1f_ln1_w", DK), ("L1f_ln1_b", DK)):
    _column(_name, _n)
NCOLS = sum(w for _, w in COLS.values())

ROWS = {n: (i * D, D) for names in (("L0x_bo", "L0a_bo", "L0f_ln2_w", "L0f_ln2_b", "L0f_gate_b"),
                                    ("L1x_bo", "L1a_bo", "L1f_ln2_w", "L1f_ln2_b")) for i, n in enumerate(names)}
NROWS1 = 4 * D
ROWS["L0f_gate_b"] = (NROWS1, 8)
ROWS["L0a_bq"] = (NROWS1 + 8, D)
ROWS["L0a_rq_b"] = (NROWS1 + 8 + D, LAT)
NROWS = NROWS1 + 8 + D + LAT

CONSTS = {}
for _name, _n in (("ident", P), ("qmask", HPG), ("scaled_qmask", HPG), ("vmask", HPG), ("fold", SEQ), ("own_batch", SEQS * 8),
                  ("group_mask", GROUPS), ("same_head", P), ("not_first", P), ("row_not_first", 1),
                  ("mask_L0a", SEQ), ("mask_L1f", SEQ), ("before", P), ("ones", P), ("countdown", 16),
                  ("multiples", TILES), ("upto", 64), ("iota", 16), ("before_own", P),
                  ("before_lower", P), ("before_upper", P), ("first_slot", 16)):
    CONSTS[_name] = (sum(w for _, w in CONSTS.values()), _n)
NCONST = sum(w for _, w in CONSTS.values())


class Chain:

    def __init__(self, eng, sem, n=0):
        self.eng, self.sem, self.n = eng, sem, n

    def link(self, ins):
        ins.then_inc(self.sem, 1)
        self.n += 1
        self.eng.wait_ge(self.sem, self.n)


def kernel_program(nc, io, out):
    ctx = ExitStack()
    with ctx:
        def sb(name, shape, dt=F32):
            return ctx.enter_context(nc.sbuf_tensor(name, shape, dt))

        def sem(name):
            return ctx.enter_context(nc.semaphore(name))

        bank = ctx.enter_context(nc.psum_tensor("bank", [P, 8, 512], F32))

        x = sb("x", [P, TILES, D])
        featT = sb("featT", [P, DK, TOK])
        qT = sb("qT", [P, DK, TOK])
        cols = sb("cols", [P, NCOLS])
        rows = sb("rows", [P, NROWS])
        consts = sb("consts", [P, NCONST])
        xw = sb("xw", [P, 4, DK, D])
        work = sb("work", [P, 5632])
        saw = sb("saw", [P, 2816])
        big = sb("big", [P, 32768])
        softmax_rows = [sb(f"softmax_{n}", [P, (GROUPS + 1) * SPT]) for n in ("max", "sum", "inverse")]
        stats = sb("stats", [P, TILES, 6])
        moments = sb("moments", [P, TILES, 2])
        rstd = sb("rstd", [P, TILES])
        minus_half = sb("minus_half", [P, TILES])
        vareps = sb("vareps", [P, TILES])

        def col(name, m=0):
            at = COLS[name][0] + m
            return cols[:, at:at + 1]

        def row(name):
            at, n = ROWS[name]
            return rows[:, at:at + n]

        def const(name):
            at, n = CONSTS[name]
            return consts[:, at:at + n]

        ident = const("ident")

        def carve(region, sizes):
            at, got = 0, []
            for n in sizes:
                got.append(region[:, at:at + n])
                at += n
            return got

        zeros = sb("zeros", [P, D])
        zeros_set = sem("zeros_set")
        zeroed = sem("zeroed")
        setup_loaded = sem("setup_loaded")

        def setup_ready(eng, L):
            eng.wait_ge(setup_loaded, 48 if L.startswith("L0") else 64)

        constants_set = sem("constants_set")
        x_loaded = sem("x_loaded")
        out_stored = sem("out_stored")

        shared = {}

        def shared_signals():
            started = {}

            def signal(name, total):
                if name not in shared:
                    shared[name] = [sem(name), 0]
                handle, count = shared[name]
                started[id(handle)] = count
                shared[name][1] += total
                return handle

            return signal, lambda handle: started[id(handle)]

        def cross_attention(L, weights, x_before, weights_before):
            (ctx_a, ctx_b, kt_a, kt_b, v_a, v_b, p_a, p_b, pt_a, pt_b, qbd_a, qbd_b, o_a, o_b,
             z_a, z_b, zt_a, zt_b, last_ctx, last_rep, vlast) = carve(
                big, [DK * CTX] * 2 + [DK * CTX] * 2 + [2 * D] * 2 + [GROUPS * CTX] * 2 + [2 * GROUPS * P] * 2
                + [DK * HPG * SEQ] * 2 + [D] * 2 + [32] * 2 + [P] * 2 + [DK * SEQS, DK * P, 4 * D])
            ctxT = [t.rearrange("p (k n) -> p k n", k=DK) for t in (ctx_a, ctx_b)]
            kT = [t.rearrange("p (k n) -> p k n", k=DK) for t in (kt_a, kt_b)]
            v = [t.rearrange("p (c n) -> p c n", c=2) for t in (v_a, v_b)]
            probs = [t.rearrange("p (g n) -> p g n", g=GROUPS) for t in (p_a, p_b)]
            probsT = [t.rearrange("p (c g n) -> p c g n", c=2, g=GROUPS) for t in (pt_a, pt_b)]
            qbd = [t.rearrange("p (m h q) -> p m h q", m=DK, h=HPG) for t in (qbd_a, qbd_b)]
            obd = [o_a, o_b]
            zlast = [z_a, z_b]
            zlastT = [zt_a, zt_b]
            last_ctx = last_ctx.rearrange("p (k s) -> p k s", k=DK)
            last_rep = last_rep.rearrange("p (k s i) -> p k s i", k=DK, i=GROUPS)
            neg_max, row_sum, inv_sum = (t[:, 0:2 * GROUPS].rearrange("p (i g) -> p i g", i=2)
                                         for t in softmax_rows)
            wq, wk, wv, wo = (xw[:, i] for i in range(4))

            signal, since = shared_signals()
            w_loaded = signal("xattn_w_loaded", 16 * len(weights))
            last_loaded = signal("xattn_last_loaded", 16)
            ctx_loaded = [signal(f"xattn_ctx_loaded{i}", 16 * SEQS // 2) for i in range(2)]
            chain_sem = signal("xattn_dve_chain", 2)
            var_ready = signal("xattn_var_ready", 1)
            rstd_ready = signal("xattn_rstd_ready", 1)
            norm_ready = signal("xattn_norm_ready", TILES)
            normT_done = signal("xattn_normT_done", TILES // 2)
            featT_ready = signal("xattn_featT_ready", TILES // 2)
            q_done = signal("xattn_q_done", 4)
            qT_ready = signal("xattn_qT_ready", 4)
            last_spread = signal("xattn_last_spread", DK)
            vlast_done = signal("xattn_vlast_done", 1)
            vlast_ready = signal("xattn_vlast_ready", 1)
            k_done = signal("xattn_k_done", SEQS)
            v_done = signal("xattn_v_done", SEQS)
            kT_ready = signal("xattn_kT_ready", SEQS)
            v_ready = signal("xattn_v_ready", SEQS)
            qbd_ready = signal("xattn_qbd_ready", SEQS)
            scores_done = signal("xattn_scores_done", GROUPS * SEQS)
            max_ready = signal("xattn_max_ready", GROUPS * SEQS)
            exp_done = signal("xattn_exp_done", GROUPS * SEQS)
            z_ready = signal("xattn_z_ready", SEQS)
            pT_done = signal("xattn_pT_done", 2 * SEQS)
            zT_done = signal("xattn_zT_done", SEQS)
            pT_ready = signal("xattn_pT_ready", 2 * SEQS)
            zT_ready = signal("xattn_zT_ready", SEQS)
            inv_ready = signal("xattn_inv_ready", SEQS)
            pv_done = signal("xattn_pv_done", SEQS)
            obd_ready = signal("xattn_obd_ready", SEQS)
            collapse_done = signal("xattn_collapse_done", SEQS)
            oT_ready = signal("xattn_oT_ready", SEQS)
            proj_done = signal("xattn_proj_done", TILES // 2)
            xbias_ready = signal("xattn_xbias_ready", TILES)
            x_done = signal("xattn_x_done", TILES // 2)

            K_BANK, V_BANK, S_BANK, T_BANK, O_BANK = 0, 2, 3, 5, 7
            bank_kT = [bank[:, K_BANK + m, 0:CTX] for m in range(DK)]
            bank_v = bank[:, V_BANK, :].rearrange("p (c n) -> p c n", c=2)
            bank_s = [bank[:, S_BANK + i, 0:CTX] for i in range(2)]
            bank_pT = [bank[:, T_BANK + c, :].rearrange("p (g n) -> p g n", g=GROUPS) for c in range(2)]
            bank_o = bank[:, O_BANK, 0:D]
            bank_zT = bank[0:32, O_BANK, 256:384]
            bank_oT = bank[:, O_BANK, 384:384 + DK * SEQ].rearrange("p (m q) -> p m q", m=DK)

            def steps(eng, step):
                step(0, 0, first=True)
                step(1, 1)
                with eng.Fori(1, SEQS // 2 - 1) as i:
                    step(2 * i, 0)
                    step(2 * i + 1, 1)
                step(SEQS - 2, 0)
                step(SEQS - 1, 1, last=True)

            def sp_weights(eng):
                weights_before(eng)
                for i, w in enumerate(weights):
                    eng.dma_start(xw[:, i], w.rearrange("(k p) n -> p k n", p=P)).then_inc(w_loaded, 16)

            def sp(eng):
                x_before(eng)
                eng.dma_start(last_ctx, io["ctx_lastT"].rearrange("(k p) s -> p k s", p=P)).then_inc(last_loaded, 16)

                def load(b, par, after=True):
                    if after:
                        eng.wait_ge(v_done, since(v_done) + b - 1)
                    eng.dma_start(ctxT[par], io["ctxT"][bass.ds(b, 1)].rearrange("o p k n -> p (o k) n")) \
                       .then_inc(ctx_loaded[par], 16)

                load(0, 0, after=False)
                load(1, 1, after=False)
                with eng.Fori(1, SEQS // 2) as i:
                    load(2 * i, 0)
                    load(2 * i + 1, 1)

            def pool(eng):
                eng.wait_ge(constants_set, 1)
                eng.wait_ge(var_ready, since(var_ready) + 1)
                eng.tensor_tensor(rstd[:], vareps[:], minus_half[:], ALU.pow).then_inc(rstd_ready, 1)
                eng.wait_ge(last_loaded, since(last_loaded) + 16)
                for k in range(DK):
                    eng.tensor_copy(last_rep[:, k], last_ctx[:, k].unsqueeze(2).broadcast_to([P, SEQS, GROUPS])) \
                       .then_inc(last_spread, 1)
                eng.wait_ge(norm_ready, since(norm_ready) + TILES)
                setup_ready(eng, L)
                for c in range(TILES):
                    eng.tensor_tensor(x[:, c], x[:, c], row(f"{L}_bo"), ALU.add).then_inc(xbias_ready, 1)

                def build_qbd(b, par, after=True):
                    if after:
                        eng.wait_ge(scores_done, since(scores_done) + 4 * b - 4)
                    eng.tensor_tensor(
                        qbd[par],
                        qT[:, :, bass.ds(b * SEQ, SEQ)].unsqueeze(2).broadcast_to([P, DK, HPG, SEQ]),
                        const("qmask").unsqueeze(1).unsqueeze(3).broadcast_to([P, DK, HPG, SEQ]),
                        ALU.mult).then_inc(qbd_ready, 1)

                eng.wait_ge(qT_ready, since(qT_ready) + 4)
                build_qbd(0, 0, after=False)

                def step(b, par, first=False, last=False):
                    if not last:
                        build_qbd(b + 1, 1 - par, after=not first)
                    eng.wait_ge(exp_done, since(exp_done) + 4 * b + 4)
                    if not first:
                        eng.wait_ge(zT_done, since(zT_done) + b - 1)
                    eng.tensor_tensor(
                        zlast[par].rearrange("p (i g) -> p i g", g=GROUPS),
                        probs[par][:, :, CTX - 1:CTX].rearrange("p g o -> p o g").broadcast_to([P, 8, GROUPS]),
                        const("own_batch")[:, bass.ds(8 * b, 8)].unsqueeze(2).broadcast_to([P, 8, GROUPS]),
                        ALU.mult).then_inc(z_ready, 1)

                steps(eng, step)

            def pe(eng):
                setup_ready(eng, L)
                for c in range(TILES):
                    eng.wait_ge(norm_ready, since(norm_ready) + c + 1)
                    for k in range(DK):
                        at = (c % 2) * DK * P + k * P
                        t = eng.transpose(bank[:, c // 2, at:at + P], featN[:, c, k * P:(k + 1) * P], ident)
                    if c % 2:
                        t.then_inc(normT_done, 1)
                eng.wait_ge(w_loaded, since(w_loaded) + 64)
                for half in range(2):
                    eng.wait_ge(featT_ready, since(featT_ready) + 2 * half + 2)
                    for m in range(DK):
                        for k in range(DK):
                            t = eng.matmul(bank[:, 4 + 2 * half + m, :], wq[:, k, m * P:(m + 1) * P],
                                           featT[:, k, half * 512:half * 512 + 512], start=k == 0, stop=k == DK - 1)
                        t.then_inc(q_done, 1)
                eng.wait_ge(last_spread, since(last_spread) + DK)
                eng.wait_ge(featT_ready, since(featT_ready) + 4)
                for s in range(4):
                    for k in range(DK):
                        t = eng.matmul(bank[0:32, s // 2, (s % 2) * D:(s % 2) * D + D],
                                       last_rep[:, k, 8 * s:8 * s + 8].rearrange("p s i -> p (s i)"), wv[:, k],
                                       start=k == 0, stop=k == DK - 1)
                t.then_inc(vlast_done, 1)

                def keys(b, par, m, first=False):
                    if m == 0:
                        eng.wait_ge(ctx_loaded[par], since(ctx_loaded[par]) + 8 * b + (16 if par == 0 else 8))
                        if first:
                            eng.wait_ge(vlast_ready, since(vlast_ready) + 1)
                        else:
                            eng.wait_ge(kT_ready, since(kT_ready) + b)
                    for k in range(DK):
                        t = eng.matmul(bank_kT[m], wk[:, k, m * P:(m + 1) * P], ctxT[par][:, k],
                                       start=k == 0, stop=k == DK - 1)
                    if m == DK - 1:
                        t.then_inc(k_done, 1)

                def values(b, par, c, first=False):
                    if c == 0 and not first:
                        eng.wait_ge(v_ready, since(v_ready) + b)
                    for k in range(DK):
                        t = eng.matmul(bank_v[:, c], ctxT[par][:, k, c * P:(c + 1) * P], wv[:, k],
                                       start=k == 0, stop=k == DK - 1)
                    if c == 1:
                        t.then_inc(v_done, 1)

                def collapse(b, par):
                    eng.wait_ge(obd_ready, since(obd_ready) + b + 1)
                    for m in range(DK):
                        t = eng.matmul(bank_oT[:, m], obd[par][:, m * P:(m + 1) * P], const("fold"),
                                       start=True, stop=True)
                    t.then_inc(collapse_done, 1)

                def scores(b, par, g, first=False):
                    if not (first and g < 2):
                        eng.wait_ge(exp_done, since(exp_done) + 4 * b + g - 1)
                    r = (g % 2) * 64
                    eng.matmul(bank_s[g % 2], qbd[par][r:r + 64, g // 2].rearrange("p h q -> p (h q)"),
                               kT[par][r:r + 64, g // 2], start=True, stop=True).then_inc(scores_done, 1)

                def step(b, par, first=False, last=False):
                    eng.wait_ge(kT_ready, since(kT_ready) + b + 1)
                    eng.wait_ge(qbd_ready, since(qbd_ready) + b + 1)
                    scores(b, par, 0, first=first)
                    scores(b, par, 1, first=first)
                    if not last:
                        keys(b + 1, 1 - par, 0)
                    if not first:
                        collapse(b - 1, 1 - par)
                    scores(b, par, 2)
                    scores(b, par, 3)
                    if not last:
                        keys(b + 1, 1 - par, 1)
                        values(b + 1, 1 - par, 0)
                    eng.wait_ge(exp_done, since(exp_done) + 4 * b + 4)
                    if not first:
                        eng.wait_ge(pT_ready, since(pT_ready) + 2 * b)
                    for c in range(2):
                        for g in range(GROUPS):
                            t = eng.transpose(bank_pT[c][:, g], probs[par][:, g, c * P:(c + 1) * P], ident)
                        t.then_inc(pT_done, 1)
                    eng.wait_ge(z_ready, since(z_ready) + b + 1)
                    if not first:
                        eng.wait_ge(oT_ready, since(oT_ready) + b)
                    eng.transpose(bank_zT, zlast[par], ident).then_inc(zT_done, 1)
                    if not last:
                        values(b + 1, 1 - par, 1)
                    eng.wait_ge(zT_ready, since(zT_ready) + b + 1)
                    eng.matmul(bank_o, zlastT[par][0:32, :], vlast[0:32, bass.ds((b // 8) * D, D)],
                               start=True, stop=False, skip_group_check=True)
                    eng.wait_ge(v_ready, since(v_ready) + b + 1)
                    for c in range(2):
                        eng.wait_ge(pT_ready, since(pT_ready) + 2 * b + c + 1)
                        for g in range(GROUPS):
                            t = eng.matmul(bank_o[:, g * 64:(g + 1) * 64], probsT[par][:, c, g],
                                           v[par][:, c, g * 64:(g + 1) * 64], start=False, stop=c == 1,
                                           skip_group_check=True)
                    t.then_inc(pv_done, 1)

                for half in range(2):
                    keys(0, 0, half, first=True)
                for half in range(2):
                    values(0, 0, half, first=True)
                steps(eng, step)
                collapse(SEQS - 1, 1)
                eng.wait_ge(oT_ready, since(oT_ready) + SEQS)
                for c in range(TILES):
                    for k in range(DK):
                        t = eng.matmul(bank[:, c // 2, (c % 2) * D:(c % 2) * D + D], featT[:, k, c * P:(c + 1) * P],
                                       wo[:, k], start=k == 0, stop=k == DK - 1)
                    if c % 2:
                        t.then_inc(proj_done, 1)

            def act(eng):
                for i in range(TILES // 2):
                    eng.wait_ge(normT_done, since(normT_done) + i + 1)
                    eng.activation(featT[:, :, 2 * i * P:(2 * i + 2) * P].rearrange("p k (c n) -> p c k n", c=2),
                                   bank[:, i, :].rearrange("p (c k n) -> p c k n", c=2, k=DK),
                                   ACT.Copy).then_inc(featT_ready, 1)

                def keys_values(b, par, first=False, again=False):
                    eng.wait_ge(k_done, since(k_done) + b + 1)
                    if not again and not first:
                        eng.wait_ge(scores_done, since(scores_done) + 4 * b - 4)
                    for m in range(DK):
                        t = eng.activation(kT[par][:, m], bank_kT[m], ACT.Identity, bias=col(f"{L}_bk", m))
                    t.then_inc(kT_ready, 1)
                    eng.wait_ge(v_done, since(v_done) + b + 1)
                    if not again and not first:
                        eng.wait_ge(pv_done, since(pv_done) + b - 1)
                    eng.activation(v[par], bank_v, ACT.Copy).then_inc(v_ready, 1)

                def out_feats(b, par, first=False):
                    eng.wait_ge(collapse_done, since(collapse_done) + b + 1)
                    for m in range(DK):
                        t = eng.activation(featT[:, m, bass.ds(b * SEQ, SEQ)], bank_oT[:, m], ACT.Identity,
                                           bias=col(f"{L}_bv", m))
                    t.then_inc(oT_ready, 1)

                def step(b, par, first=False, last=False):
                    for g in range(GROUPS):
                        eng.wait_ge(max_ready, since(max_ready) + 4 * b + g + 1)
                        if g == 0 and not first:
                            eng.wait_ge(pT_done, since(pT_done) + 2 * b - 2)
                            eng.wait_ge(z_ready, since(z_ready) + b - 1)
                            eng.wait_ge(inv_ready, since(inv_ready) + b - 1)
                        eng.activation(probs[par][:, g], bank_s[g % 2], ACT.Exp, bias=neg_max[:, par, g:g + 1],
                                       accum_out=row_sum[:, par, g:g + 1]).then_inc(exp_done, 1)
                    if not first:
                        out_feats(b - 1, 1 - par)
                    if not last:
                        keys_values(b + 1, 1 - par, again=first)

                setup_ready(eng, L)
                keys_values(0, 0, first=True)
                steps(eng, step)
                out_feats(SEQS - 1, 1)

            def dve(eng):
                chain = Chain(eng, chain_sem, since(chain_sem))
                x_before(eng)
                for c in range(TILES):
                    t = eng.bn_stats(stats[:, c], x[:, c])
                chain.link(t)
                for c in range(TILES):
                    t = eng.bn_aggr(moments[:, c], stats[:, c])
                chain.link(t)
                eng.tensor_scalar(vareps[:], moments[:, :, 1], EPS, None, ALU.add).then_inc(var_ready, 1)
                eng.wait_ge(rstd_ready, since(rstd_ready) + 1)
                for c in range(TILES):
                    eng.tensor_scalar(featN[:, c], x[:, c], moments[:, c, 0:1], rstd[:, c:c + 1],
                                      ALU.subtract, ALU.mult).then_inc(norm_ready, 1)
                setup_ready(eng, L)
                eng.wait_ge(normT_done, since(normT_done) + TILES // 2)
                for n in range(4):
                    half, m = divmod(n, 2)
                    eng.wait_ge(q_done, since(q_done) + n + 1)
                    eng.tensor_scalar(qT[:, m, half * 512:half * 512 + 512], bank[:, 4 + n, :], col(f"{L}_bq", m),
                                      HD ** -0.5, ALU.add, ALU.mult).then_inc(qT_ready, 1)
                eng.wait_ge(vlast_done, since(vlast_done) + 1)
                eng.tensor_tensor(vlast[0:32].rearrange("p (s g n) -> p s g n", s=4, g=GROUPS),
                                  bank[0:32, 0:2, :].rearrange("p a (b g n) -> p (a b) g n", b=2, g=GROUPS),
                                  const("group_mask")[0:32].unsqueeze(1).unsqueeze(3)
                                  .broadcast_to([32, 4, GROUPS, D // GROUPS]),
                                  ALU.mult).then_inc(vlast_ready, 1)

                def build_obd(b, par):
                    eng.wait_ge(pv_done, since(pv_done) + b + 1)
                    if not isinstance(b, int) or b >= 2:
                        eng.wait_ge(collapse_done, since(collapse_done) + b - 1)
                    eng.wait_ge(inv_ready, since(inv_ready) + b + 1)
                    for g in range(GROUPS):
                        t = eng.scalar_tensor_tensor(
                            obd[par][:, g * 64:(g + 1) * 64].rearrange("p (h n) -> p h n", h=HPG),
                            bank_o[:, g * 64:(g + 1) * 64].rearrange("p (h n) -> p h n", h=HPG),
                            inv_sum[:, par, g:g + 1],
                            const("vmask").unsqueeze(2).broadcast_to([P, HPG, HD]), ALU.mult, ALU.mult)
                    t.then_inc(obd_ready, 1)

                def step(b, par, first=False, last=False):
                    if not first:
                        build_obd(b - 1, 1 - par)
                    for g in range(GROUPS):
                        eng.wait_ge(scores_done, since(scores_done) + 4 * b + g + 1)
                        if g == 0 and not first:
                            eng.wait_ge(exp_done, since(exp_done) + 4 * b - 4)
                        eng.tensor_reduce(neg_max[:, par, g:g + 1], bank_s[g % 2], AX.X, ALU.max, negate=True) \
                           .then_inc(max_ready, 1)
                    eng.wait_ge(exp_done, since(exp_done) + 4 * b + 4)
                    if not first:
                        eng.wait_ge(obd_ready, since(obd_ready) + b)
                    eng.reciprocal(inv_sum[:, par], row_sum[:, par]).then_inc(inv_ready, 1)
                    for c in range(2):
                        eng.wait_ge(pT_done, since(pT_done) + 2 * b + c + 1)
                        if not first:
                            eng.wait_ge(pv_done, since(pv_done) + b - 1)
                        eng.tensor_copy(probsT[par][:, c], bank_pT[c]).then_inc(pT_ready, 1)
                        if c == 0:
                            eng.wait_ge(zT_done, since(zT_done) + b + 1)
                            eng.tensor_copy(zlastT[par][0:32, :], bank_zT).then_inc(zT_ready, 1)

                steps(eng, step)
                build_obd(SEQS - 1, 1)
                eng.wait_ge(xbias_ready, since(xbias_ready) + TILES)
                for i in range(TILES // 2):
                    eng.wait_ge(proj_done, since(proj_done) + i + 1)
                    pair = x[:, 2 * i:2 * i + 2].rearrange("p c n -> p (c n)")
                    eng.tensor_tensor(pair, bank[:, i, :], pair, ALU.add).then_inc(x_done, 1)

            featN = qT[:].rearrange("p k (c n) -> p (k c) n", n=D)

            def x_after(eng):
                eng.wait_ge(x_done, since(x_done) + TILES // 2)

            return dict(sp=sp, sp_weights=sp_weights, pool=pool, pe=pe, act=act, dve=dve), x_after

        def norm_tokens(L, src, dst, before, more=()):
            signal, since = shared_signals()
            chain_sem = signal("norm_chain", 2)
            var_ready = signal("norm_var_ready", 1)
            rstd_ready = signal("norm_rstd_ready", 1)
            done = signal("norm_done", TILES)

            def pool(eng):
                eng.wait_ge(constants_set, 1)
                eng.wait_ge(var_ready, since(var_ready) + 1)
                eng.tensor_tensor(rstd[:], vareps[:], minus_half[:], ALU.pow).then_inc(rstd_ready, 1)

            def dve(eng):
                chain = Chain(eng, chain_sem, since(chain_sem))
                before(eng)
                for c in range(TILES):
                    t = eng.bn_stats(stats[:, c], src[:, c])
                chain.link(t)
                for c in range(TILES):
                    t = eng.bn_aggr(moments[:, c], stats[:, c])
                chain.link(t)
                eng.tensor_scalar(vareps[:], moments[:, :, 1], EPS, None, ALU.add).then_inc(var_ready, 1)
                eng.wait_ge(rstd_ready, since(rstd_ready) + 1)
                for c in range(TILES):
                    eng.tensor_scalar(dst[:, c], src[:, c], moments[:, c, 0:1], rstd[:, c:c + 1],
                                      ALU.subtract, ALU.mult).then_inc(done, 1)

            def after(eng, tiles=TILES):
                eng.wait_ge(done, since(done) + tiles)

            return dict(pool=pool, dve=dve), after

        def self_attention(L, src, dst, weights, w_qkv, w_out, before, mask=None, ln=None, bias=True,
                           latent=None, spread_kv=None, out_bias=None, load_after=lambda eng: None):
            NG = GROUPS + (1 if latent else 0)
            LINKS = 5 if latent else 4
            NB = NG * SPT
            (hN, hT, hT4, kT, qbd, vbd, probs, probsT, oT) = carve(
                work, [D, D, 4 * D, D, 4 * D, 4 * D, NB * SEQ, NB * SEQ, D])
            hT4 = hT4.rearrange("p (k j n) -> p k j n", k=DK, j=SPT)
            hT = hT.rearrange("p (k n) -> p k n", k=DK)
            kT = kT.rearrange("p (m n) -> p m n", m=DK)
            qbd = qbd.rearrange("p (a h q) -> p a h q", h=HPG, q=SEQ)
            vbd = vbd.rearrange("p (j g n) -> p j g n", j=SPT, g=GROUPS)
            s3 = probs.rearrange("p (a k) -> p a k", k=SEQ)
            row_max, row_sum, inv_sum = (t[:, 0:NB] for t in softmax_rows)
            NEVEN = NB - 2 * SPT

            def block_at(g, j):
                return (NEVEN if g % 2 else 0) + (g // 2) * SPT + j
            oT = oT.rearrange("p (m n) -> p m n", m=DK)
            if latent:
                rq_w, rkv_w, rout_w, gate_l = latent
                (r_kT, r_qbd, r_vbd, latT, remT, gateT, mixT, gate_r) = carve(
                    big[:, 32768 - 2048:], [P, 4 * P, SPT * LAT, P, D, D, D, P])
                r_qbd = r_qbd.rearrange("p (j h q) -> p j h q", j=SPT, h=HPG)
                r_vbd = r_vbd.rearrange("p (j n) -> p j n", j=SPT)
                remT = remT.rearrange("p (m n) -> p m n", m=DK)
                gateT = gateT.rearrange("p (m n) -> p m n", m=DK)
                mixT = mixT.rearrange("p (m n) -> p m n", m=DK)
            outT = mixT if latent else oT

            signal, since = shared_signals()
            w_loaded = sem(f"{L}_w_loaded")
            if spread_kv:
                kv_spread = sem(f"{L}_kv_spread")
            if out_bias is not None:
                bias_added = sem(f"{L}_bias_added")
            hN_ready = signal("attn_hN_ready", TILES)
            nT_done = signal("attn_nT_done", TILES)
            hT_ready = signal("attn_hT_ready", TILES)
            hT4_ready = signal("attn_hT4_ready", TILES)
            qk_done = signal("attn_qk_done", TILES)
            vrep_done = signal("attn_vrep_done", TILES)
            kT_ready = signal("attn_kT_ready", TILES)
            qbd_ready = signal("attn_qbd_ready", TILES)
            vbd_ready = signal("attn_vbd_ready", TILES)
            scores_done = signal("attn_scores_done", TILES)
            softmax_chain = signal("attn_softmax_chain", LINKS * TILES)
            scores_out = signal("attn_scores_out", TILES)
            shifted_ready = signal("attn_shifted_ready", TILES)
            exp_done = signal("attn_exp_done", TILES)
            pT_ready = signal("attn_pT_ready", TILES)
            pv_done = signal("attn_pv_done", TILES)
            oT_ready = signal("attn_oT_ready", TILES)
            out_done = signal("attn_out_done", TILES)
            x_done = signal("attn_x_done", TILES)

            if latent:
                gate_w_ready = sem(f"{L}_gate_w_ready")
                rem_done = sem(f"{L}_rem_done")
                remT_ready = sem(f"{L}_remT_ready")
                gate_done = sem(f"{L}_gate_done")
                gateT_ready = sem(f"{L}_gateT_ready")
                mix_chain = sem(f"{L}_mix_chain")
                mixT_ready = sem(f"{L}_mixT_ready")

            bank_nT = bank[:, 0, 0:D].rearrange("p (k n) -> p k n", k=DK)
            bank_k = bank_nT
            bank_rk = bank[0:LAT, 0, D:D + P]
            bank_q = bank[:, 1, 0:D].rearrange("p (m n) -> p m n", m=DK)
            bank_rq = bank[0:LAT, 1, D:D + P]
            bank_v = bank[:, 2:4, :].rearrange("p a (j n) -> p (a j) n", j=2)
            bank_s = [bank[:, 4, 0:NEVEN * SEQ], bank[:, 5, 0:2 * SPT * SEQ]]

            def scores_to(g, j):
                at = (g // 2) * SPT + j
                return bank_s[g % 2][:, at * SEQ:(at + 1) * SEQ]
            bank_rv = bank[:, 5, D:2 * D].rearrange("p (j n) -> p j n", j=SPT)
            bank_oT = bank[:, 6, 0:D].rearrange("p (m n) -> p m n", m=DK)
            bank_lat = bank[0:LAT, 6, D:D + P]
            bank_rem = bank[:, 7, 0:D].rearrange("p (m n) -> p m n", m=DK)
            bank_gate = bank[:, 7, D:2 * D].rearrange("p (m n) -> p m n", m=DK)
            bank_out = bank[:, 7, 0:D]

            def steps(eng, step):
                step(0, first=True)
                step(1, second=True)
                with eng.Fori(2, TILES - 1) as c:
                    step(c)
                step(TILES - 1, last=True)

            def sp(eng):
                load_after(eng)
                for dram, tile in weights:
                    eng.dma_start(tile, dram).then_inc(w_loaded, 16)

            def pool(eng):
                def stage_in(c, wait=True):
                    if wait:
                        eng.wait_ge(nT_done, since(nT_done) + c)
                    eng.tensor_copy(hN, src[:, bass.ds(c, 1)].rearrange("p o n -> p (o n)")).then_inc(hN_ready, 1)

                before(eng, 1)
                stage_in(0, wait=False)
                if spread_kv:
                    narrow, nq = spread_kv
                    eng.wait_ge(w_loaded, 16 * len(weights))
                    for k in range(DK):
                        for i in range(2):
                            eng.tensor_copy(
                                w_qkv[:, k, (i + 1) * D:(i + 2) * D].rearrange("p (g r d) -> p g r d", g=GROUPS, r=HPG),
                                narrow[:, k, nq + i * LAT:nq + (i + 1) * LAT].rearrange("p (g d) -> p g d", g=GROUPS)
                                .unsqueeze(2).broadcast_to([P, GROUPS, HPG, HD])).then_inc(kv_spread, 1)
                        eng.tensor_copy(w_qkv[:, k, 0:D], narrow[:, k, 0:nq]).then_inc(kv_spread, 1)
                before(eng)
                if out_bias is not None:
                    for c in range(TILES):
                        eng.tensor_tensor(dst[:, c], dst[:, c], out_bias, ALU.add).then_inc(bias_added, 1)
                if latent:
                    setup_ready(eng, L)
                    for w, v in ((gate_l, "L0a_gl"), (gate_r, "L0a_gr")):
                        eng.tensor_tensor(w, const("same_head"), col(v).broadcast_to([P, P]), ALU.mult) \
                           .then_inc(gate_w_ready, 1)
                stage_in(1)
                with eng.Fori(2, TILES) as c:
                    stage_in(c)

            def pe(eng):
                def transposes(c, first=False):
                    eng.wait_ge(hN_ready, since(hN_ready) + c + 1)
                    if not first:
                        eng.wait_ge(kT_ready, since(kT_ready) + c)
                    for k in range(DK):
                        t = eng.transpose(bank_nT[:, k], hN[:, k * P:(k + 1) * P], ident)
                    t.then_inc(nT_done, 1)

                def queries_keys(c, first=False):
                    eng.wait_ge(hT_ready, since(hT_ready) + c + 1)
                    if not first:
                        eng.wait_ge(qbd_ready, since(qbd_ready) + c)
                    if latent:
                        for k in range(DK):
                            eng.matmul(bank_rq, rq_w[:, k, 0:LAT], hT[:, k], start=k == 0, stop=False)
                        eng.matmul(bank_rq, row("L0a_rq_b")[0:1], const("ones")[0:1], start=False, stop=True)
                    for m in range(DK):
                        for k in range(DK):
                            eng.matmul(bank_q[:, m], w_qkv[:, k, m * P:(m + 1) * P], hT[:, k],
                                       start=k == 0, stop=k == DK - 1 and not bias)
                        if bias:
                            eng.matmul(bank_q[:, m], row(f"{L}_bq")[0:1, m * P:(m + 1) * P], const("ones")[0:1],
                                       start=False, stop=True)
                    eng.wait_ge(hT4_ready, since(hT4_ready) + c + 1)
                    if latent:
                        for k in range(DK):
                            eng.matmul(bank_rk, rkv_w[:, k, 0:LAT], hT[:, k], start=k == 0, stop=k == DK - 1)
                    for m in range(DK):
                        for k in range(DK):
                            t = eng.matmul(bank_k[:, m], w_qkv[:, k, D + m * P:D + (m + 1) * P], hT[:, k],
                                           start=k == 0, stop=k == DK - 1)
                    t.then_inc(qk_done, 1)

                def values(c, first=False):
                    if not first:
                        eng.wait_ge(vbd_ready, since(vbd_ready) + c)
                    for j in range(SPT):
                        for k in range(DK):
                            t = eng.matmul(bank_v[:, j], hT4[:, k, j], w_qkv[:, k, 2 * D:3 * D],
                                           start=k == 0, stop=k == DK - 1)
                    if latent:
                        eng.wait_ge(scores_out, since(scores_out) + c + 1)
                        for j in range(SPT):
                            for k in range(DK):
                                t = eng.matmul(bank_rv[:, j], hT4[:, k, j], rkv_w[:, k, LAT:2 * LAT],
                                               start=k == 0, stop=k == DK - 1)
                    t.then_inc(vrep_done, 1)

                def scores(c, first=False):
                    eng.wait_ge(qbd_ready, since(qbd_ready) + c + 1)
                    eng.wait_ge(kT_ready, since(kT_ready) + c + 1)
                    if not first:
                        eng.wait_ge(scores_out, since(scores_out) + c)
                        if latent:
                            eng.wait_ge(vbd_ready, since(vbd_ready) + c)
                    for g in range(GROUPS):
                        r = (g % 2) * LAT
                        for j in range(SPT):
                            t = eng.matmul(scores_to(g, j),
                                           qbd[r:r + LAT, (g // 2) * SPT + j].rearrange("p h q -> p (h q)"),
                                           kT[r:r + LAT, g // 2, j * SEQ:(j + 1) * SEQ], start=True, stop=True)
                    if latent:
                        for j in range(SPT):
                            t = eng.matmul(scores_to(GROUPS, j), r_qbd[0:LAT, j].rearrange("p h q -> p (h q)"),
                                           r_kT[0:LAT, j * SEQ:(j + 1) * SEQ], start=True, stop=True)
                    t.then_inc(scores_done, 1)

                def weigh(c, first=False):
                    eng.wait_ge(pT_ready, since(pT_ready) + c + 1)
                    eng.wait_ge(vbd_ready, since(vbd_ready) + c + 1)
                    if not first:
                        eng.wait_ge(oT_ready, since(oT_ready) + c)
                    for g in range(GROUPS):
                        r = (g % 2) * LAT
                        for j in range(SPT):
                            at = block_at(g, j) * SEQ
                            t = eng.matmul(bank_oT[r:r + LAT, g // 2, j * SEQ:(j + 1) * SEQ], vbd[:, j, g],
                                           probsT[:, at:at + SEQ], start=True, stop=True)
                    if latent:
                        for j in range(SPT):
                            at = block_at(GROUPS, j) * SEQ
                            t = eng.matmul(bank_lat[:, j * SEQ:(j + 1) * SEQ], r_vbd[:, j],
                                           probsT[:, at:at + SEQ], start=True, stop=True)
                    t.then_inc(pv_done, 1)

                def remote(c, first=False):
                    eng.wait_ge(oT_ready, since(oT_ready) + c + 1)
                    if not first:
                        eng.wait_ge(x_done, since(x_done) + c)
                    for m in range(DK):
                        t = eng.matmul(bank_rem[:, m], rout_w[0:LAT, m * P:(m + 1) * P], latT[0:LAT], start=True,
                                       stop=True)
                    t.then_inc(rem_done, 1)

                def gate(c):
                    eng.wait_ge(remT_ready, c + 1)
                    for m in range(DK):
                        eng.matmul(bank_gate[:, m], gate_l, oT[:, m], start=True, stop=False)
                        t = eng.matmul(bank_gate[:, m], gate_r, remT[:, m], start=False, stop=True)
                    t.then_inc(gate_done, 1)

                def output(c, first=False):
                    if latent:
                        eng.wait_ge(mixT_ready, c + 1)
                    else:
                        eng.wait_ge(oT_ready, since(oT_ready) + c + 1)
                        if not first:
                            eng.wait_ge(x_done, since(x_done) + c)
                    for k in range(DK):
                        t = eng.matmul(bank_out, outT[:, k], w_out[:, k], start=k == 0, stop=k == DK - 1)
                    t.then_inc(out_done, 1)

                def step(c, first=False, second=False, last=False):
                    scores(c, first=first)
                    if latent and not first:
                        remote(c - 1, first=second)
                    if not last:
                        transposes(c + 1)
                    if not latent and not first:
                        output(c - 1)
                    values(c, first=first)
                    if latent and not first:
                        gate(c - 1)
                    if not last:
                        queries_keys(c + 1)
                    if latent and not first:
                        output(c - 1)
                    weigh(c, first=first)

                eng.wait_ge(w_loaded, 16 * len(weights))
                if spread_kv:
                    eng.wait_ge(kv_spread, 3 * DK)
                if latent:
                    eng.wait_ge(gate_w_ready, 2)
                transposes(0, first=True)
                queries_keys(0, first=True)
                steps(eng, step)
                if latent:
                    remote(TILES - 1)
                    gate(TILES - 1)
                output(TILES - 1)

            def act(eng):
                def feats(c, first=False):
                    eng.wait_ge(nT_done, since(nT_done) + c + 1)
                    if not first:
                        eng.wait_ge(qk_done, since(qk_done) + c)
                    for k in range(DK):
                        w, b = (col(ln[0], k), col(ln[1], k)) if ln else (1.0, 0.0)
                        t = eng.activation(hT[:, k], bank_nT[:, k], ACT.Identity, scale=w, bias=b)
                    t.then_inc(hT_ready, 1)

                def feats_four_times(c, first=False):
                    if not first:
                        eng.wait_ge(vrep_done, since(vrep_done) + c)
                    for k in range(DK):
                        w, b = (col(ln[0], k), col(ln[1], k)) if ln else (1.0, 0.0)
                        t = eng.activation(hT4[:, k].rearrange("p j (h q) -> p j h q", h=HPG),
                                           bank_nT[:, k].rearrange("p (j q) -> p j q", j=SPT).unsqueeze(2)
                                           .broadcast_to([P, SPT, HPG, SEQ]), ACT.Identity, scale=w, bias=b)
                    t.then_inc(hT4_ready, 1)

                def own_values(c, first=False):
                    eng.wait_ge(vrep_done, since(vrep_done) + c + 1)
                    if not first:
                        eng.wait_ge(pv_done, since(pv_done) + c)
                    for h in range(HPG):
                        t = eng.activation(vbd.rearrange("p j g (h d) -> p (j g) h d", h=HPG)[:, :, h],
                                           bank_v.rearrange("p j (g h d) -> p (j g) h d", g=GROUPS, h=HPG)[:, :, h],
                                           ACT.Copy, scale=const("vmask")[:, h:h + 1])
                        if latent:
                            t = eng.activation(r_vbd.rearrange("p j (h d) -> p j h d", h=HPG)[:, :, h],
                                               bank_rv.rearrange("p j (h d) -> p j h d", h=HPG)[:, :, h],
                                               ACT.Copy, scale=const("vmask")[:, h:h + 1])
                    t.then_inc(vbd_ready, 1)

                def keys(c, first=False):
                    eng.wait_ge(qk_done, since(qk_done) + c + 1)
                    if not first:
                        eng.wait_ge(scores_done, since(scores_done) + c)
                    for m in range(DK):
                        t = eng.activation(kT[:, m], bank_k[:, m], ACT.Identity,
                                           bias=col(f"{L}_bk", m) if bias else 0.0)
                    if latent:
                        t = eng.activation(r_kT[0:LAT], bank_rk, ACT.Identity, bias=col("L0a_rkq_b")[0:LAT])
                    t.then_inc(kT_ready, 1)

                def heads_out(c, first=False):
                    eng.wait_ge(pv_done, since(pv_done) + c + 1)
                    if not first:
                        eng.wait_ge(out_done, since(out_done) + c)
                    eng.activation(oT, bank_oT, ACT.Copy).then_inc(oT_ready, 1)

                def remote_out(c):
                    eng.wait_ge(rem_done, c + 1)
                    for m in range(DK):
                        t = eng.activation(remT[:, m], bank_rem[:, m], ACT.Identity, bias=col("L0a_rout_b", m))
                    t.then_inc(remT_ready, 1)

                def gate_out(c):
                    eng.wait_ge(gate_done, c + 1)
                    eng.activation(gateT, bank_gate, ACT.Tanh, scale=0.5).then_inc(gateT_ready, 1)

                def exps(c):
                    eng.wait_ge(shifted_ready, since(shifted_ready) + c + 1)
                    eng.activation(probs, probs, ACT.Exp).then_inc(exp_done, 1)

                def step(c, first=False, second=False, last=False):
                    if latent and not first:
                        remote_out(c - 1)
                    if not last:
                        feats(c + 1)
                    exps(c)
                    if not last:
                        feats_four_times(c + 1)
                    if latent and not first:
                        gate_out(c - 1)
                    own_values(c, first=first)
                    if not last:
                        keys(c + 1)
                    if not latent:
                        heads_out(c, first=first)

                setup_ready(eng, L)
                feats(0, first=True)
                feats_four_times(0, first=True)
                keys(0, first=True)
                steps(eng, step)
                if latent:
                    remote_out(TILES - 1)
                    gate_out(TILES - 1)

            def dve(eng):
                def softmax(c, first=False):
                    at = [LINKS * c]

                    def link(ins):
                        ins.then_inc(softmax_chain, 1)
                        at[0] = at[0] + 1
                        eng.wait_ge(softmax_chain, since(softmax_chain) + at[0])

                    eng.wait_ge(scores_done, since(scores_done) + c + 1)
                    for blocks, scores in ((slice(0, NEVEN), bank_s[0]), (slice(NEVEN, NB), bank_s[1])):
                        scores = scores.rearrange("p (a k) -> p a k", k=SEQ)
                        if mask:
                            t = eng.tensor_tensor(s3[:, blocks], scores, const(mask).unsqueeze(1)
                                                  .broadcast_to([P, scores.shape[1], SEQ]), ALU.add)
                        else:
                            t = eng.tensor_copy(s3[:, blocks], scores)
                    link(t)
                    eng.tensor_reduce(row_max[:], s3, AX.X, ALU.max).then_inc(scores_out, 1)
                    eng.wait_ge(scores_out, since(scores_out) + c + 1)
                    eng.tensor_tensor(s3, s3, row_max[:].unsqueeze(2).broadcast_to([P, NB, SEQ]), ALU.subtract) \
                       .then_inc(shifted_ready, 1)
                    eng.wait_ge(exp_done, since(exp_done) + c + 1)
                    link(eng.tensor_reduce(row_sum[:], s3, AX.X, ALU.add))
                    link(eng.reciprocal(inv_sum[:], row_sum[:]))
                    if latent:
                        link(eng.tensor_scalar(inv_sum[:], inv_sum[:], const("row_not_first"), None, ALU.mult))
                    link(eng.tensor_tensor(s3, s3, inv_sum[:].unsqueeze(2).broadcast_to([P, NB, SEQ]), ALU.mult))
                    if not first:
                        eng.wait_ge(pv_done, since(pv_done) + c)
                    eng.transpose(probsT, probs).then_inc(pT_ready, 1)

                def build_qbd(c, first=False):
                    eng.wait_ge(qk_done, since(qk_done) + c + 1)
                    if not first:
                        eng.wait_ge(scores_done, since(scores_done) + c)
                    parts = [(qbd[:, 4 * m:4 * m + 4], bank_q[:, m], P) for m in range(DK)]
                    if latent:
                        parts.append((r_qbd[0:LAT], bank_rq, LAT))
                    for to, queries, n in parts:
                        t = eng.tensor_tensor(
                            to, queries.rearrange("p (j q) -> p j q", j=SPT).unsqueeze(2)
                            .broadcast_to([n, SPT, HPG, SEQ]),
                            const("scaled_qmask")[0:n].unsqueeze(1).unsqueeze(3).broadcast_to([n, SPT, HPG, SEQ]),
                            ALU.mult)
                    t.then_inc(qbd_ready, 1)

                def heads_out(c, first=False):
                    eng.wait_ge(pv_done, since(pv_done) + c + 1)
                    for m in range(DK):
                        eng.scalar_tensor_tensor(oT[:, m], const("not_first"), col(f"{L}_bv", m), bank_oT[:, m],
                                                 ALU.mult, ALU.add)
                    eng.scalar_tensor_tensor(latT[0:LAT], const("not_first")[0:LAT], col("L0a_rv_b")[0:LAT], bank_lat,
                                             ALU.mult, ALU.add).then_inc(oT_ready, 1)

                def mix(c, first=False):
                    at = [3 * c]

                    def link(ins):
                        ins.then_inc(mix_chain, 1)
                        at[0] = at[0] + 1
                        eng.wait_ge(mix_chain, at[0])

                    eng.wait_ge(remT_ready, c + 1)
                    if not first:
                        eng.wait_ge(out_done, since(out_done) + c)
                    link(eng.tensor_tensor(mixT, oT, remT, ALU.subtract))
                    eng.wait_ge(gateT_ready, c + 1)
                    link(eng.tensor_scalar(gateT, gateT, 0.5, 0.5, ALU.mult, ALU.add))
                    link(eng.tensor_tensor(mixT, mixT, gateT, ALU.mult))
                    eng.tensor_tensor(mixT, mixT, remT, ALU.add).then_inc(mixT_ready, 1)

                def add_output(c):
                    eng.wait_ge(out_done, since(out_done) + c + 1)
                    to = dst[:, bass.ds(c, 1)].rearrange("p o n -> p (o n)")
                    eng.tensor_tensor(to, bank_out, to, ALU.add).then_inc(x_done, 1)

                def step(c, first=False, second=False, last=False):
                    softmax(c, first=first)
                    if latent and not first:
                        mix(c - 1, first=second)
                    if not last:
                        build_qbd(c + 1)
                    if not first:
                        add_output(c - 1)
                    if latent:
                        heads_out(c)

                before(eng)
                setup_ready(eng, L)
                build_qbd(0, first=True)
                if out_bias is not None:
                    eng.wait_ge(bias_added, TILES)
                steps(eng, step)
                if latent:
                    mix(TILES - 1)
                add_output(TILES - 1)

            def x_after(eng):
                eng.wait_ge(x_done, since(x_done) + TILES)

            return dict(sp=sp, pool=pool, pe=pe, act=act, dve=dve), x_after

        def experts_top1(L, tok, normed, wb, gate_w, gate_b, before):
            scr_in, scr_out = io["scratch_in0"], io["scratch_out0"]
            E, HID, NBLK = 8, 1024, TILES + 8 - 1
            hT = work[:, 0:DK * TOK].rearrange("p (k n) -> p k n", k=DK)
            (block_in, block_inT, hid, hidT, block_out, back) = carve(work, [D, D, HID, HID, D, TILES * D])
            block_inT = block_inT.rearrange("p (k n) -> p k n", k=DK)
            hidT = hidT.rearrange("p (k n) -> p k n", k=HID // P)
            back = back.rearrange("p (c n) -> p c n", c=TILES)
            w_norm, b_norm = wb

            def small(name, shape, dt=F32):
                return sb(f"{L}_{name}", [P] + shape, dt)

            gw = small("gate_w", [DK, E])
            logits = small("logits", [TILES, E])
            best = small("best", [TILES])
            onehot = small("onehot", [TILES, E])
            cmp = small("cmp", [16 * E])
            count = small("count", [E])
            n_blocks = small("n_blocks", [E])
            block_end = small("block_end", [E])
            slot_f = small("slot_f", [TILES])
            slot = small("slot", [TILES], U32)
            owner_f = small("owner_f", [NBLK])
            owner = small("owner", [NBLK], I32)

            gate_loaded = sem(f"{L}_gate_loaded")
            chain_sem = sem(f"{L}_chain")
            scaled_ready = sem(f"{L}_scaled_ready")
            sT_done = sem(f"{L}_sT_done")
            hT_ready = sem(f"{L}_hT_ready")
            logits_done = sem(f"{L}_logits_done")
            onehot_ready = sem(f"{L}_onehot_ready")
            ranks_done = sem(f"{L}_ranks_done")
            slot_ready = sem(f"{L}_slot_ready")
            owner_ready = sem(f"{L}_owner_ready")
            scattered = sem(f"{L}_scattered")
            in_loaded = sem(f"{L}_in_loaded")
            inT_done = sem(f"{L}_inT_done")
            inT_ready = sem(f"{L}_inT_ready")
            up_done = sem(f"{L}_up_done")
            hid_ready = sem(f"{L}_hid_ready")
            hidT_done = sem(f"{L}_hidT_done")
            hidT_ready = sem(f"{L}_hidT_ready")
            down_done = sem(f"{L}_down_done")
            out_ready = sem(f"{L}_out_ready")
            out_kept = sem(f"{L}_out_kept")
            x_done = sem(f"{L}_x_done")

            bank_inT = bank[:, 0, 0:D].rearrange("p (k n) -> p k n", k=DK)
            bank_up = [bank[:, 1 + i, :] for i in range(2)]
            bank_hT = [bank[:, 3 + i, :].rearrange("p (k n) -> p k n", k=4) for i in range(2)]
            bank_down = bank[:, 5, 0:D]

            def steps(eng, step):
                step(0, first=True)
                with eng.Fori(1, NBLK - 1) as b:
                    step(b)
                step(NBLK - 1, last=True)

            def sp(eng):
                eng.dma_start(gw[:], gate_w).then_inc(gate_loaded, 16)

                def load(b, wait=True):
                    if wait:
                        eng.wait_ge(inT_done, b)
                    eng.dma_start(block_in, scr_in[bass.ds(b * P, P), :]).then_inc(in_loaded, 16)

                eng.wait_ge(scattered, 16 * TILES)
                load(0, wait=False)
                with eng.Fori(1, NBLK) as b:
                    load(b)

            def pool(eng):
                eng.wait_ge(zeroed, 32)
                for c in range(TILES):
                    eng.wait_ge(slot_ready, 1)
                    eng.indirect_dma_start(scr_in, bass.IndirectOffsetOnAxis(ap=slot[:, c:c + 1], axis=0),
                                           normed[:, c], None, bounds_check=NBLK * P - 1,
                                           oob_is_err=False).then_inc(scattered, 16)

                def keep(b):
                    eng.wait_ge(out_ready, b + 1)
                    eng.dma_start(scr_out[bass.ds(b * P, P), :], block_out).then_inc(out_kept, 16)

                keep(0)
                with eng.Fori(1, NBLK) as b:
                    keep(b)
                eng.wait_ge(out_kept, 16 * NBLK)
                for c in range(TILES):
                    eng.indirect_dma_start(back[:, c], None, scr_out,
                                           bass.IndirectOffsetOnAxis(ap=slot[:, c:c + 1], axis=0),
                                           bounds_check=NBLK * P - 1, oob_is_err=False).then_inc(gathered[c // 4], 16)

            gathered = [sem(f"{L}_gathered{i}") for i in range(2)]

            def pe(eng):
                for i in range(TILES // 2):
                    eng.wait_ge(scaled_ready, 2)
                    for c in range(2):
                        for k in range(DK):
                            at = (c * DK + k) * P
                            t = eng.transpose(bank[:, i, at:at + P], normed[:, 2 * i + c, k * P:(k + 1) * P], ident)
                    t.then_inc(sT_done, 1)
                eng.wait_ge(gate_loaded, 16)
                for c in range(TILES):
                    eng.wait_ge(hT_ready, c // 2 + 1)
                    for k in range(DK):
                        t = eng.matmul(bank[:, 4, c * E:(c + 1) * E], hT[:, k, c * P:(c + 1) * P], gw[:, k],
                                       start=k == 0, stop=k == DK - 1)
                t.then_inc(logits_done, 1)
                eng.wait_ge(onehot_ready, 1)
                flat = onehot[:].rearrange("p c e -> p (c e)")
                eng.matmul(bank[:, 5, 0:TILES * E], const("before"), flat, start=True, stop=False,
                           skip_group_check=True)
                for d in range(1, TILES):
                    t = eng.matmul(bank[:, 5, d * E:TILES * E], const("ones"), flat[:, 0:(TILES - d) * E],
                                   start=False, stop=d == TILES - 1, skip_group_check=True)
                for c in range(TILES):
                    t = eng.matmul(bank[:, 6, 0:E], const("ones"), onehot[:, c], start=c == 0, stop=c == TILES - 1)
                t.then_inc(ranks_done, 1)

                def transpose_in(b, first=False):
                    eng.wait_ge(in_loaded, 16 * b + 16)
                    for k in range(DK):
                        t = eng.transpose(bank_inT[:, k], block_in[:, k * P:(k + 1) * P], ident)
                    t.then_inc(inT_done, 1)

                def expert(b):
                    return eng.value_load(owner[0:1, bass.ds(b, 1)], min_val=0, max_val=E - 1)

                def up(b, e, first=False):
                    eng.wait_ge(inT_ready, b + 1)
                    if not first:
                        eng.wait_ge(hid_ready, b)
                    for i in range(2):
                        for k in range(DK):
                            t = eng.matmul(bank_up[i], block_inT[:, k],
                                           big[:, bass.ds(e * (DK * HID) + k * HID + i * 512, 512)],
                                           start=k == 0, stop=k == DK - 1)
                    t.then_inc(up_done, 1)

                def transpose_hidden(b, first=False):
                    eng.wait_ge(hid_ready, b + 1)
                    if not first:
                        eng.wait_ge(hidT_ready, b)
                    for k in range(HID // P):
                        t = eng.transpose(bank_hT[k // 4][:, k % 4], hid[:, k * P:(k + 1) * P], ident)
                    t.then_inc(hidT_done, 1)

                def down(b, e, first=False):
                    eng.wait_ge(hidT_ready, b + 1)
                    if not first:
                        eng.wait_ge(out_ready, b)
                    for k in range(HID // P):
                        t = eng.matmul(bank_down, hidT[:, k], big[:, bass.ds(e * (HID // P * D) + 16384 + k * D, D)],
                                       start=k == 0, stop=k == HID // P - 1)
                    t.then_inc(down_done, 1)

                def step(b, first=False, last=False):
                    own = expert(b)
                    if not last:
                        following = expert(b + 1)
                        transpose_in(b + 1)
                    transpose_hidden(b, first=first)
                    if not last:
                        up(b + 1, following)
                    down(b, own, first=first)

                eng.wait_ge(owner_ready, 1)
                eng.wait_ge(experts_loaded, 16 * 16)
                transpose_in(0, first=True)
                up(0, expert(0), first=True)
                steps(eng, step)

            def act(eng):
                for i in range(TILES // 2):
                    eng.wait_ge(sT_done, i + 1)
                    eng.activation(hT[:, :, 2 * i * P:(2 * i + 2) * P].rearrange("p k (c n) -> p c k n", c=2),
                                   bank[:, i, :].rearrange("p (c k n) -> p c k n", c=2, k=DK),
                                   ACT.Copy).then_inc(hT_ready, 1)

                def gelu(b, first=False):
                    eng.wait_ge(up_done, b + 1)
                    if not first:
                        eng.wait_ge(hidT_done, b)
                    for i in range(2):
                        t = eng.activation(hid[:, i * 512:(i + 1) * 512], bank_up[i], ACT.Gelu_apprx_tanh)
                    t.then_inc(hid_ready, 1)

                gelu(0, first=True)
                gelu(1)
                with eng.Fori(2, NBLK) as b:
                    gelu(b)

            def dve(eng):
                chain = Chain(eng, chain_sem)
                before(eng)
                chain.link(eng.tensor_tensor(normed, normed, w_norm.unsqueeze(1).broadcast_to([P, TILES, D]),
                                             ALU.mult))
                eng.tensor_tensor(normed, normed, b_norm.unsqueeze(1).broadcast_to([P, TILES, D]), ALU.add) \
                   .then_inc(scaled_ready, 2)
                chain.link(eng.tensor_tensor(x[:], x[:], tok, ALU.add))
                eng.wait_ge(logits_done, 1)
                chain.link(eng.tensor_tensor(logits[:], bank[:, 4, 0:TILES * E].rearrange("p (c e) -> p c e", e=E),
                                             gate_b.unsqueeze(1).broadcast_to([P, TILES, E]), ALU.add))
                chain.link(eng.tensor_reduce(best[:], logits[:], AX.X, ALU.max))
                chain.link(eng.tensor_tensor(onehot[:], logits[:], best[:].unsqueeze(2).broadcast_to([P, TILES, E]),
                                             ALU.is_equal))
                chain.link(eng.tensor_tensor(logits[:], onehot[:], const("countdown")[:, 8:16].unsqueeze(1)
                                             .broadcast_to([P, TILES, E]), ALU.mult))
                chain.link(eng.tensor_reduce(best[:], logits[:], AX.X, ALU.max))
                eng.tensor_tensor(onehot[:], logits[:], best[:].unsqueeze(2).broadcast_to([P, TILES, E]),
                                  ALU.is_equal).then_inc(onehot_ready, 1)
                eng.wait_ge(onehot_ready, 1)
                eng.wait_ge(ranks_done, 1)
                chain.link(eng.tensor_copy(count[:], bank[:, 6, 0:E]))
                grid = cmp[:, 0:E * TILES].rearrange("p (e j) -> p e j", e=E)
                chain.link(eng.tensor_tensor(grid, count[:].unsqueeze(2).broadcast_to([P, E, TILES]),
                                             const("multiples").unsqueeze(1).broadcast_to([P, E, TILES]),
                                             ALU.is_gt))
                chain.link(eng.tensor_reduce(n_blocks[:], grid, AX.X, ALU.add))
                upto = cmp[:, 0:E * E].rearrange("p (f e) -> p f e", e=E)
                chain.link(eng.tensor_tensor(upto, n_blocks[:].unsqueeze(1).broadcast_to([P, E, E]),
                                             const("upto").rearrange("p (f e) -> p f e", e=E), ALU.mult))
                chain.link(eng.tensor_reduce(block_end[:], upto, AX.X, ALU.add))
                ended = cmp[:, 0:NBLK * E].rearrange("p (b e) -> p b e", e=E)
                chain.link(eng.tensor_tensor(ended, block_end[:].unsqueeze(1).broadcast_to([P, NBLK, E]),
                                             const("iota")[:, 0:NBLK].unsqueeze(2).broadcast_to([P, NBLK, E]),
                                             ALU.is_le))
                chain.link(eng.tensor_reduce(owner_f[:], ended, AX.X, ALU.add))
                eng.tensor_scalar(owner[:], owner_f[:], float(E - 1), None, ALU.min).then_inc(owner_ready, 1)
                chain.link(eng.tensor_tensor(block_end[:], block_end[:], n_blocks[:], ALU.subtract))
                chain.link(eng.tensor_scalar(block_end[:], block_end[:], float(P), None, ALU.mult))
                chain.link(eng.tensor_tensor(logits[:], bank[:, 5, 0:TILES * E].rearrange("p (c e) -> p c e", e=E),
                                             block_end[:].unsqueeze(1).broadcast_to([P, TILES, E]), ALU.add))
                chain.link(eng.tensor_tensor(logits[:], logits[:], onehot[:], ALU.mult))
                chain.link(eng.tensor_reduce(slot_f[:], logits[:], AX.X, ALU.add))
                eng.tensor_copy(slot[:], slot_f[:]).then_inc(slot_ready, 1)

                def rows_in(b, first=False):
                    eng.wait_ge(inT_done, b + 1)
                    if not first:
                        eng.wait_ge(up_done, b)
                    eng.tensor_copy(block_inT, bank_inT).then_inc(inT_ready, 1)

                def hidden(b, first=False):
                    eng.wait_ge(hidT_done, b + 1)
                    if not first:
                        eng.wait_ge(down_done, b)
                    for i in range(2):
                        t = eng.tensor_copy(hidT[:, 4 * i:4 * i + 4], bank_hT[i])
                    t.then_inc(hidT_ready, 1)

                def rows_out(b, first=False):
                    eng.wait_ge(down_done, b + 1)
                    if not first:
                        eng.wait_ge(out_kept, 16 * b)
                    eng.tensor_copy(block_out, bank_down).then_inc(out_ready, 1)

                def step(b, first=False, last=False):
                    if not last:
                        rows_in(b + 1)
                    hidden(b, first=first)
                    rows_out(b, first=first)

                rows_in(0, first=True)
                steps(eng, step)
                for c in range(TILES):
                    if c % 4 == 0:
                        eng.wait_ge(gathered[c // 4], 16 * 4)
                    eng.tensor_tensor(x[:, c], x[:, c], back[:, c], ALU.add).then_inc(x_done, 1)

            def x_after(eng):
                eng.wait_ge(x_done, TILES)

            return dict(sp=sp, pool=pool, pe=pe, act=act, dve=dve), x_after

        def wide_attention(L, src, emb, before, load_after, banks_free):
            INNER, WHD = 1024, 64
            M = INNER // P
            SC = 512
            (wq, wkv, wo) = carve(big[:, 16384:], [DK * INNER, DK * 2 * INNER, M * D])
            wq, wkv = (t.rearrange("p (k n) -> p k n", k=DK) for t in (wq, wkv))
            wo = wo.rearrange("p (k n) -> p k n", k=M)
            buckets = big[0:32, 24576:28672].rearrange("p (k n) -> p k n", k=SEQ)
            probsT, rel_bias = carve(big[:, 28672:], [HEADS * P, HEADS * SEQ])
            probsT = probsT.rearrange("p (a n) -> p a n", a=HEADS)
            rel_bias = rel_bias.rearrange("p (a k) -> p a k", k=SEQ)
            (hN, hT, qT_w, kT_w, v_w, probs, oT) = carve(work, [D, D, INNER, INNER, INNER, HEADS * SEQ, INNER])
            hT = hT.rearrange("p (k n) -> p k n", k=DK)
            qT_w, kT_w, oT = (t.rearrange("p (m n) -> p m n", m=M) for t in (qT_w, kT_w, oT))
            s3 = probs.rearrange("p (a k) -> p a k", k=SEQ)
            row_max, row_sum, inv_sum = (t[:, 0:HEADS] for t in softmax_rows)
            emb_sb = sb(f"{L}_emb", [32, HEADS])

            w_loaded = sem(f"{L}_w_loaded")
            bias_added = sem(f"{L}_bias_added")
            blocks_cleared = sem(f"{L}_blocks_cleared")
            rel_done = sem(f"{L}_rel_done")
            rel_ready = sem(f"{L}_rel_ready")
            hN_ready = sem(f"{L}_hN_ready")
            nT_done = sem(f"{L}_nT_done")
            hT_ready = sem(f"{L}_hT_ready")
            part_done = sem(f"{L}_part_done")
            part_out = sem(f"{L}_part_out")
            scores_done = sem(f"{L}_scores_done")
            softmax_chain = sem(f"{L}_softmax_chain")
            scores_out = sem(f"{L}_scores_out")
            shifted_ready = sem(f"{L}_shifted_ready")
            exp_done = sem(f"{L}_exp_done")
            pT_ready = sem(f"{L}_pT_ready")
            pv_done = sem(f"{L}_pv_done")
            oT_ready = sem(f"{L}_oT_ready")
            out_done = sem(f"{L}_out_done")
            x_done = sem(f"{L}_x_done")

            bank_nT = bank[:, 0, 0:D].rearrange("p (k n) -> p k n", k=DK)
            bank_part = [bank[:, 1 + i, :] for i in range(2)]
            bank_s = [bank[:, 3 + i, 0:D] for i in range(2)]
            bank_oT = bank[:, 5:7, :].rearrange("p a (m n) -> p (a m) n", n=P)
            bank_out = bank[:, 7, 0:D]
            PARTS = 6

            def steps(eng, step):
                step(0, first=True)
                with eng.Fori(1, TILES - 1) as c:
                    step(c)
                step(TILES - 1, last=True)

            def sp(eng):
                load_after(eng)
                for dram, tile in ((w_rows("L1_attn_Wq"), wq), (w_rows("L1_attn_Wkv"), wkv),
                                   (io["L1_attn_Wo"].rearrange("(k p) n -> p k n", p=P), wo),
                                   (io["buckets"].rearrange("b (k n) -> b k n", k=SEQ), buckets), (emb, emb_sb[:])):
                    eng.dma_start(tile, dram).then_inc(w_loaded, 16)

            def pool(eng):
                def stage_in(c, wait=True):
                    if wait:
                        eng.wait_ge(nT_done, c)
                    eng.tensor_copy(hN, src[:, bass.ds(c, 1)].rearrange("p o n -> p (o n)")).then_inc(hN_ready, 1)

                before(eng, 1)
                stage_in(0, wait=False)
                eng.memset(probsT, 0.0).then_inc(blocks_cleared, 1)
                setup_ready(eng, L)
                before(eng)
                for c in range(TILES):
                    eng.tensor_tensor(x[:, c], x[:, c], row(f"{L}_bo"), ALU.add).then_inc(bias_added, 1)
                with eng.Fori(1, TILES) as c:
                    stage_in(c)

            def pe(eng):
                eng.wait_ge(w_loaded, 80)
                banks_free(eng)
                for k in range(SEQ):
                    t = eng.matmul(bank[:, 3, k * HEADS:(k + 1) * HEADS], buckets[:, k], emb_sb[:], start=True,
                                   stop=True)
                t.then_inc(rel_done, 1)

                def transposes(c):
                    eng.wait_ge(hN_ready, c + 1)
                    for k in range(DK):
                        t = eng.transpose(bank_nT[:, k], hN[:, k * P:(k + 1) * P], ident)
                    t.then_inc(nT_done, 1)

                def project(c, first=False):
                    eng.wait_ge(hT_ready, c + 1)
                    for u in range(PARTS):
                        if not first or u >= 2:
                            eng.wait_ge(part_out, PARTS * c + u - 1)
                        to = bank_part[u % 2]
                        if u < 4:
                            w = (wq, wkv)[u // 2]
                            for m in range(4):
                                at = (4 * (u % 2) + m) * P
                                for k in range(DK):
                                    t = eng.matmul(to[:, m * P:(m + 1) * P], w[:, k, at:at + P], hT[:, k],
                                                   start=k == 0, stop=k == DK - 1)
                        else:
                            at = INNER + (u - 4) * SC
                            for k in range(DK):
                                t = eng.matmul(to, hT[:, k], wkv[:, k, at:at + SC], start=k == 0, stop=k == DK - 1)
                        t.then_inc(part_done, 1)

                def scores(c, first=False):
                    if first:
                        eng.wait_ge(rel_ready, 1)
                    for h in range(HEADS):
                        r = (h % 2) * WHD
                        for j in range(SPT):
                            t = eng.matmul(bank_s[h % 2][j * SEQ:(j + 1) * SEQ, (h // 2) * SEQ:(h // 2 + 1) * SEQ],
                                           qT_w[r:r + WHD, h // 2, j * SEQ:(j + 1) * SEQ],
                                           kT_w[r:r + WHD, h // 2, j * SEQ:(j + 1) * SEQ], start=True, stop=True)
                    t.then_inc(scores_done, 1)

                def weigh(c, first=False):
                    eng.wait_ge(pT_ready, c + 1)
                    eng.wait_ge(part_out, PARTS * c + 6)
                    if not first:
                        eng.wait_ge(oT_ready, c)
                    for h in range(HEADS):
                        r = (h % 2) * WHD
                        t = eng.matmul(bank_oT[r:r + WHD, h // 2], v_w[:, h * WHD:(h + 1) * WHD],
                                       probsT[:, (h % 2) * 8 + h // 2], start=True, stop=True)
                    t.then_inc(pv_done, 1)

                def output(c, first=False):
                    eng.wait_ge(oT_ready, c + 1)
                    if not first:
                        eng.wait_ge(x_done, c)
                    for k in range(M):
                        t = eng.matmul(bank_out, oT[:, k], wo[:, k], start=k == 0, stop=k == M - 1)
                    t.then_inc(out_done, 1)

                transposes(0)
                project(0, first=True)
                scores(0, first=True)
                transposes(1)
                project(1)
                weigh(0, first=True)
                scores(1)
                transposes(2)
                output(0, first=True)
                project(2)
                weigh(1)
                scores(2)
                with eng.Fori(2, TILES - 1) as c:
                    transposes(c + 1)
                    output(c - 1)
                    project(c + 1)
                    weigh(c)
                    scores(c + 1)
                output(TILES - 2)
                weigh(TILES - 1)
                output(TILES - 1)

            def act(eng):
                def feats(c, first=False):
                    eng.wait_ge(nT_done, c + 1)
                    if not first:
                        eng.wait_ge(part_done, PARTS * c)
                    eng.activation(hT, bank_nT, ACT.Copy).then_inc(hT_ready, 1)

                def parts(c, first=False):
                    for u in range(PARTS):
                        eng.wait_ge(part_done, PARTS * c + u + 1)
                        if u == 0 and not first:
                            eng.wait_ge(scores_done, c)
                        if u == 4 and not first:
                            eng.wait_ge(pv_done, c)
                        to = ((qT_w, kT_w)[u // 2][:, 4 * (u % 2):4 * (u % 2) + 4].rearrange("p m n -> p (m n)")
                              if u < 4 else v_w[:, (u - 4) * SC:(u - 3) * SC])
                        eng.activation(to, bank_part[u % 2], ACT.Copy,
                                       scale=WHD ** -0.5 if u < 2 else 1.0).then_inc(part_out, 1)

                def exps(c):
                    eng.wait_ge(shifted_ready, c + 1)
                    eng.activation(probs, probs, ACT.Exp).then_inc(exp_done, 1)

                def heads_out(c, first=False):
                    eng.wait_ge(pv_done, c + 1)
                    if not first:
                        eng.wait_ge(out_done, c)
                    for i in range(2):
                        t = eng.activation(oT[:, 4 * i:4 * i + 4], bank_oT[:, 4 * i:4 * i + 4], ACT.Copy)
                    t.then_inc(oT_ready, 1)

                def step(c, first=False, last=False):
                    if not last:
                        feats(c + 1)
                        parts(c + 1)
                    heads_out(c, first=first)
                    if not last:
                        exps(c + 1)

                feats(0, first=True)
                parts(0, first=True)
                exps(0)
                steps(eng, step)

            def dve(eng):
                before(eng)
                eng.wait_ge(rel_done, 1)
                for i in range(2):
                    t = eng.tensor_copy(rel_bias[:, 8 * i:8 * i + 8],
                                        bank[:, 3, :].rearrange("p (k a i) -> p i a k", i=2, a=8)[:, i])
                t.then_inc(rel_ready, 1)
                eng.wait_ge(rel_ready, 1)

                def softmax(c, first=False):
                    at = [4 * c]

                    def link(ins):
                        ins.then_inc(softmax_chain, 1)
                        at[0] = at[0] + 1
                        eng.wait_ge(softmax_chain, at[0])

                    eng.wait_ge(scores_done, c + 1)
                    for i in range(2):
                        heads = slice(8 * i, 8 * i + 8)
                        t = eng.tensor_tensor(s3[:, heads], bank_s[i].rearrange("p (a k) -> p a k", k=SEQ),
                                              rel_bias[:, heads], ALU.add)
                    link(t)
                    eng.tensor_reduce(row_max[:], s3, AX.X, ALU.max).then_inc(scores_out, 1)
                    eng.wait_ge(scores_out, c + 1)
                    eng.tensor_tensor(s3, s3, row_max[:].unsqueeze(2).broadcast_to([P, HEADS, SEQ]), ALU.subtract) \
                       .then_inc(shifted_ready, 1)
                    eng.wait_ge(exp_done, c + 1)
                    link(eng.tensor_reduce(row_sum[:], s3, AX.X, ALU.add))
                    link(eng.reciprocal(inv_sum[:], row_sum[:]))
                    link(eng.tensor_tensor(s3, s3, inv_sum[:].unsqueeze(2).broadcast_to([P, HEADS, SEQ]), ALU.mult))
                    if first:
                        eng.wait_ge(blocks_cleared, 1)
                    else:
                        eng.wait_ge(pv_done, c)
                    for j in range(SPT):
                        own = slice(j * SEQ, (j + 1) * SEQ)
                        t = eng.transpose(probsT[own, :, own], s3[own])
                    t.then_inc(pT_ready, 1)

                def add_output(c):
                    eng.wait_ge(out_done, c + 1)
                    to = x[:, bass.ds(c, 1)].rearrange("p o n -> p (o n)")
                    eng.tensor_tensor(to, bank_out, to, ALU.add).then_inc(x_done, 1)

                def step(c, first=False, last=False):
                    if not first:
                        add_output(c - 1)
                    if not last:
                        softmax(c + 1)

                softmax(0, first=True)
                eng.wait_ge(bias_added, TILES)
                steps(eng, step)
                add_output(TILES - 1)

            def x_after(eng, tiles=TILES):
                eng.wait_ge(x_done, tiles)

            return dict(sp=sp, pool=pool, pe=pe, act=act, dve=dve), x_after

        def experts_top2(L, tok, normed, wb, router, before, load_after):
            scr_in, scr_out = io["scratch_in1"], io["scratch_out1"]
            E, HID, CAP, HALF = 16, 512, 160, 80
            ROWS_E = E * CAP
            KH = HID // P
            BEYOND = 1e6
            hT = work[:, 0:DK * TOK].rearrange("p (k n) -> p k n", k=DK)
            (rows_in, rows_inT, hidT, w_up, rows_out, back1) = carve(
                work, [2 * D, DK * CAP, KH * CAP, DK * HID, 2 * D, TILES * D])
            rows_in, rows_out = (t.rearrange("p (i n) -> p i n", i=2) for t in (rows_in, rows_out))
            rows_inT = rows_inT.rearrange("p (k n) -> p k n", k=DK)
            hidT = hidT.rearrange("p (k n) -> p k n", k=KH)
            back = [back1.rearrange("p (c n) -> p c n", c=TILES),
                    xw[:].rearrange("p i k n -> p (i k) n")]
            w_norm, b_norm = wb

            def small(name, shape, dt=F32):
                return sb(f"{L}_{name}", [P] + shape, dt)

            gw = small("router", [DK, E])
            probs, scratch, onehot0, onehot1, chosen = (
                t.rearrange("p (c e) -> p c e", e=E) for t in carve(saw, [TILES * E] * 5))
            onehot = [onehot0, onehot1]
            best = small("best", [TILES])
            top = [small(f"top{i}", [TILES]) for i in range(2)]
            rank = small("rank", [TILES])
            keep = small("keep", [TILES])
            slot_f = small("slot_f", [TILES])
            slot_to = [small(f"slot_to{i}", [TILES], U32) for i in range(2)]
            slot_from = [small(f"slot_from{i}", [TILES], U32) for i in range(2)]

            gate_loaded = sem(f"{L}_gate_loaded")
            w_loaded = sem(f"{L}_w_loaded")
            chain_sem = sem(f"{L}_chain")
            scaled_ready = sem(f"{L}_scaled_ready")
            sT_done = sem(f"{L}_sT_done")
            hT_ready = sem(f"{L}_hT_ready")
            logits_done = sem(f"{L}_logits_done")
            shifted_ready = sem(f"{L}_shifted_ready")
            exp_done = sem(f"{L}_exp_done")
            chosen_ready = sem(f"{L}_chosen_ready")
            ranks_done = sem(f"{L}_ranks_done")
            slot_ready = sem(f"{L}_slot_ready")
            scattered = sem(f"{L}_scattered")
            in_loaded = sem(f"{L}_in_loaded")
            inT_done = sem(f"{L}_inT_done")
            inT_ready = sem(f"{L}_inT_ready")
            w_up_ready = sem(f"{L}_w_up_ready")
            up_done = sem(f"{L}_up_done")
            hid_ready = sem(f"{L}_hid_ready")
            down_done = sem(f"{L}_down_done")
            out_ready = sem(f"{L}_out_ready")
            out_kept = sem(f"{L}_out_kept")
            gathered = [sem(f"{L}_gathered{i}") for i in range(2)]
            add_chain = sem(f"{L}_add_chain")
            x_done = sem(f"{L}_x_done")

            bank_inT = bank[:, 0, 0:DK * CAP].rearrange("p (k n) -> p k n", k=DK)
            bank_up = [bank[:, 1 + i, 0:2 * CAP].rearrange("p (m n) -> p m n", m=2) for i in range(2)]
            bank_down = bank[0:HALF, 3, :].rearrange("p (i n) -> p i n", i=2)

            def expert_rows(dram, e):
                return dram[bass.ds(e * CAP, CAP), :].rearrange("(i p) n -> p i n", p=HALF)

            def steps(eng, step):
                step(0, first=True)
                with eng.Fori(1, E - 1) as e:
                    step(e)
                step(E - 1, last=True)

            def sp_weights(eng):
                load_after(eng)
                eng.dma_start(gw[:], router).then_inc(gate_loaded, 16)
                for i, (name, k) in enumerate((("L1_ffn_w1T", DK), ("L1_ffn_w2T", KH))):
                    for e in range(0, E, 2):
                        at = i * 16384 + e * 1024
                        eng.dma_start(big[:, at:at + 2048].rearrange("p (e k n) -> p e k n", e=2, k=k),
                                      io[name][e:e + 2].rearrange("e (k p) n -> p e k n", p=P)).then_inc(w_loaded, 16)

            def sp(eng):
                def load(e, wait=True):
                    if wait:
                        eng.wait_ge(inT_done, e)
                    eng.dma_start(rows_in[0:HALF], expert_rows(scr_in, e)).then_inc(in_loaded, 16)

                eng.wait_ge(scattered, 16 * 2 * TILES)
                load(0, wait=False)
                with eng.Fori(1, E) as e:
                    load(e)

            def pool(eng):
                eng.wait_ge(zeroed, 32)
                for i in range(2):
                    eng.wait_ge(slot_ready, i + 1)
                    for c in range(TILES):
                        eng.indirect_dma_start(scr_in, bass.IndirectOffsetOnAxis(ap=slot_to[i][:, c:c + 1], axis=0),
                                               normed[:, c], None, bounds_check=ROWS_E - 1,
                                               oob_is_err=False).then_inc(scattered, 16)

                def keep_rows(e):
                    eng.wait_ge(out_ready, e + 1)
                    eng.dma_start(expert_rows(scr_out, e), rows_out[0:HALF]).then_inc(out_kept, 16)

                keep_rows(0)
                with eng.Fori(1, E) as e:
                    keep_rows(e)
                eng.wait_ge(out_kept, 16 * E)
                for c in range(TILES):
                    for i in range(2):
                        eng.indirect_dma_start(back[i][:, c], None, scr_out,
                                               bass.IndirectOffsetOnAxis(ap=slot_from[i][:, c:c + 1], axis=0),
                                               bounds_check=ROWS_E - 1,
                                               oob_is_err=False).then_inc(gathered[c // 4], 16)

            def pe(eng):
                eng.wait_ge(scaled_ready, 2)
                for i in range(TILES // 2):
                    for c in range(2):
                        for k in range(DK):
                            at = (c * DK + k) * P
                            t = eng.transpose(bank[:, i, at:at + P], normed[:, 2 * i + c, k * P:(k + 1) * P], ident)
                    t.then_inc(sT_done, 1)
                eng.wait_ge(gate_loaded, 16)
                for c in range(TILES):
                    eng.wait_ge(hT_ready, c // 2 + 1)
                    for k in range(DK):
                        t = eng.matmul(bank[:, 4, c * E:(c + 1) * E], hT[:, k, c * P:(c + 1) * P], gw[:, k],
                                       start=k == 0, stop=k == DK - 1)
                t.then_inc(logits_done, 1)
                eng.wait_ge(chosen_ready, 1)
                flat = chosen.rearrange("p c e -> p (c e)")
                ranks = bank[:, 5, 0:TILES * E]
                eng.matmul(ranks, const("before_own"), flat, start=True, stop=False, skip_group_check=True)
                for d in range(1, TILES):
                    n = (TILES - d) * E
                    eng.matmul(ranks[:, d * E:], const("before_lower"), flat[:, 0:n], start=False, stop=False,
                               skip_group_check=True)
                    t = eng.matmul(ranks[:, 0:n], const("before_upper"), flat[:, d * E:], start=False,
                                   stop=d == TILES - 1, skip_group_check=True)
                t.then_inc(ranks_done, 1)

                def transpose_in(e, first=False):
                    eng.wait_ge(in_loaded, 16 * e + 16)
                    for i in range(2):
                        for k in range(DK):
                            t = eng.transpose(bank_inT[:, k, i * HALF:(i + 1) * HALF],
                                              rows_in[0:HALF, i, k * P:(k + 1) * P], ident[0:HALF, 0:HALF])
                    t.then_inc(inT_done, 1)

                def up(e, first=False):
                    eng.wait_ge(inT_ready, e + 1)
                    eng.wait_ge(w_up_ready, e + 1)
                    for i in range(2):
                        if not first:
                            eng.wait_ge(hid_ready, 2 * e + i - 1)
                        for m in range(2):
                            at = (2 * i + m) * P
                            for k in range(DK):
                                t = eng.matmul(bank_up[i][:, m], w_up3[:, k, at:at + P], rows_inT[:, k],
                                               start=k == 0, stop=k == DK - 1)
                        t.then_inc(up_done, 1)

                def down(e, first=False):
                    if not first:
                        eng.wait_ge(out_ready, e)
                    for i in range(2):
                        for k in range(KH):
                            if i == 0 and k % 2 == 0:
                                eng.wait_ge(hid_ready, 2 * e + 1 + k // 2)
                            t = eng.matmul(bank_down[:, i], hidT[:, k, i * HALF:(i + 1) * HALF],
                                           big[:, bass.ds(e * (KH * D) + 16384 + k * D, D)],
                                           start=k == 0, stop=k == KH - 1)
                    t.then_inc(down_done, 1)

                def step(e, first=False, last=False):
                    if not last:
                        transpose_in(e + 1)
                    down(e, first=first)
                    if not last:
                        up(e + 1)

                eng.wait_ge(w_loaded, 16 * E)
                transpose_in(0, first=True)
                up(0, first=True)
                steps(eng, step)

            def act(eng):
                for i in range(TILES // 2):
                    eng.wait_ge(sT_done, i + 1)
                    eng.activation(hT[:, :, 2 * i * P:(2 * i + 2) * P].rearrange("p k (c n) -> p c k n", c=2),
                                   bank[:, i, :].rearrange("p (c k n) -> p c k n", c=2, k=DK),
                                   ACT.Copy).then_inc(hT_ready, 1)
                eng.wait_ge(shifted_ready, 1)
                eng.activation(probs, probs, ACT.Exp).then_inc(exp_done, 1)

                def gelu(e, first=False):
                    for i in range(2):
                        eng.wait_ge(up_done, 2 * e + i + 1)
                        if i == 0 and not first:
                            eng.wait_ge(down_done, e)
                        eng.activation(hidT[:, 2 * i:2 * i + 2], bank_up[i], ACT.Gelu_apprx_tanh) \
                           .then_inc(hid_ready, 1)

                gelu(0, first=True)
                with eng.Fori(1, E) as e:
                    gelu(e)

            def dve(eng):
                chain = Chain(eng, chain_sem)
                before(eng)
                setup_ready(eng, L)
                chain.link(eng.tensor_tensor(normed, normed, w_norm.unsqueeze(1).broadcast_to([P, TILES, D]),
                                             ALU.mult))
                eng.tensor_tensor(normed, normed, b_norm.unsqueeze(1).broadcast_to([P, TILES, D]), ALU.add) \
                   .then_inc(scaled_ready, 2)
                chain.link(eng.tensor_tensor(x[:], x[:], tok, ALU.add))

                def over_experts(v):
                    return v.unsqueeze(2).broadcast_to([P, TILES, E])

                def over_tiles(v):
                    return v.unsqueeze(1).broadcast_to([P, TILES, E])

                eng.wait_ge(logits_done, 1)
                logits = bank[:, 4, 0:TILES * E].rearrange("p (c e) -> p c e", e=E)
                chain.link(eng.tensor_reduce(best[:], logits, AX.X, ALU.max))
                eng.tensor_tensor(probs, logits, over_experts(best[:]), ALU.subtract).then_inc(shifted_ready, 1)
                eng.wait_ge(exp_done, 1)
                chain.link(eng.tensor_reduce(best[:], probs, AX.X, ALU.add))
                chain.link(eng.reciprocal(best[:], best[:]))
                chain.link(eng.tensor_tensor(probs, probs, over_experts(best[:]), ALU.mult))
                for i in range(2):
                    chain.link(eng.tensor_reduce(top[i][:], probs, AX.X, ALU.max))
                    chain.link(eng.tensor_tensor(onehot[i], probs, over_experts(top[i][:]), ALU.is_equal))
                    chain.link(eng.tensor_tensor(scratch, onehot[i], over_tiles(const("countdown")), ALU.mult))
                    chain.link(eng.tensor_reduce(best[:], scratch, AX.X, ALU.max))
                    chain.link(eng.tensor_tensor(onehot[i], scratch, over_experts(best[:]), ALU.is_equal))
                    if i == 0:
                        chain.link(eng.scalar_tensor_tensor(
                            probs.rearrange("p c e -> p (c e)"), onehot[0].rearrange("p c e -> p (c e)"), -2.0,
                            probs.rearrange("p c e -> p (c e)"), ALU.mult, ALU.add))
                eng.tensor_tensor(chosen, onehot[0], onehot[1], ALU.add).then_inc(chosen_ready, 1)
                eng.wait_ge(ranks_done, 1)
                ranks = bank[:, 5, 0:TILES * E].rearrange("p (c e) -> p c e", e=E)
                for i in range(2):
                    chain.link(eng.tensor_tensor(scratch, ranks, onehot[i], ALU.mult))
                    chain.link(eng.tensor_reduce(rank[:], scratch, AX.X, ALU.add))
                    chain.link(eng.tensor_scalar(keep[:], rank[:], float(CAP), None, ALU.is_lt))
                    chain.link(eng.tensor_tensor(top[i][:], top[i][:], keep[:], ALU.mult))
                    chain.link(eng.tensor_tensor(scratch, onehot[i], over_tiles(const("first_slot")), ALU.mult))
                    chain.link(eng.tensor_reduce(slot_f[:], scratch, AX.X, ALU.add))
                    chain.link(eng.tensor_tensor(slot_f[:], slot_f[:], rank[:], ALU.add))
                    eng.tensor_scalar(slot_from[i][:], slot_f[:], float(ROWS_E - 1), None, ALU.min)
                    chain.link(eng.tensor_scalar(keep[:], keep[:], -BEYOND, BEYOND, ALU.mult, ALU.add))
                    eng.tensor_tensor(slot_to[i][:], slot_f[:], keep[:], ALU.add).then_inc(slot_ready, 1)
                    eng.wait_ge(slot_ready, i + 1)

                def features_in(e, first=False):
                    if not first:
                        eng.wait_ge(up_done, 2 * e)
                    eng.tensor_copy(w_up, big[:, bass.ds(e * (DK * HID), DK * HID)]).then_inc(w_up_ready, 1)
                    eng.wait_ge(inT_done, e + 1)
                    eng.tensor_copy(rows_inT, bank_inT).then_inc(inT_ready, 1)

                def rows_back(e, first=False):
                    eng.wait_ge(down_done, e + 1)
                    if not first:
                        eng.wait_ge(out_kept, 16 * e)
                    eng.tensor_copy(rows_out[0:HALF], bank_down).then_inc(out_ready, 1)

                def step(e, first=False, last=False):
                    if not last:
                        features_in(e + 1)
                    rows_back(e, first=first)

                eng.wait_ge(w_loaded, 16 * E)
                features_in(0, first=True)
                steps(eng, step)
                for c in range(TILES):
                    if c % 4 == 0:
                        eng.wait_ge(gathered[c // 4], 16 * 4 * 2)
                    eng.scalar_tensor_tensor(x[:, c], back[0][:, c], top[0][:, c:c + 1], x[:, c], ALU.mult,
                                             ALU.add).then_inc(add_chain, 1)
                    eng.wait_ge(add_chain, c + 1)
                    eng.scalar_tensor_tensor(x[:, c], back[1][:, c], top[1][:, c:c + 1], x[:, c], ALU.mult,
                                             ALU.add).then_inc(x_done, 1)

            w_up3 = w_up.rearrange("p (k n) -> p k n", k=DK)

            def x_after(eng):
                eng.wait_ge(x_done, TILES)

            return dict(sp=sp, sp_weights=sp_weights, pool=pool, pe=pe, act=act, dve=dve), x_after

        def x_start(eng):
            eng.wait_ge(x_loaded, 16)

        layers = []

        def add(made):
            layers.append(made[0])
            return made[1]

        def w_rows(name):
            return io[name].rearrange("(k p) n -> p k n", p=P)

        tokA = featT[:].rearrange("p k (c n) -> p (k c) n", n=D)
        tokB = qT[:].rearrange("p k (c n) -> p (k c) n", n=D)
        L0x, after_L0x = cross_attention("L0x", [io["L0_xattn_" + w] for w in ("Wq", "Wk", "Wv", "Wo")], x_start,
                                         lambda eng: None)
        layers += [dict(sp=L0x.pop("sp_weights")), L0x]

        def zero_scratch(eng):
            eng.wait_ge(zeros_set, 1)
            for name in ("scratch_in0", "scratch_in1"):
                n = io[name].shape[0] // P
                eng.dma_start(io[name].rearrange("(b p) n -> p b n", p=P),
                              zeros[:].unsqueeze(1).broadcast_to([P, n, D])).then_inc(zeroed, 16)

        layers.append(dict(pool=zero_scratch))
        after = add(norm_tokens("L0a_norm", x, tokA, after_L0x))
        w_qkv, w_out, rq_w, rkv_w, rout_w, gate_l = carve(saw, [DK * 3 * D, DK * D, DK * LAT, DK * 2 * LAT, D, P])
        w_qkv, w_out, rq_w, rkv_w = (t.rearrange("p (k n) -> p k n", k=DK) for t in (w_qkv, w_out, rq_w, rkv_w))
        after_L0a = add(self_attention(
            "L0a", tokA, x,
            [(w_rows("L0_attn_qkv_w"), w_qkv), (w_rows("L0_attn_out_w"), w_out), (w_rows("L0_attn_rq_w"), rq_w),
             (w_rows("L0_attn_rkv_w"), rkv_w), (io["L0_attn_rout_w"], rout_w[0:LAT])],
            w_qkv, w_out, after, mask="mask_L0a", latent=(rq_w, rkv_w, rout_w, gate_l), out_bias=row("L0a_bo")))

        experts_loaded = sem("experts_loaded")

        def load_experts(eng):
            after_L0x(eng)
            for e in range(8):
                eng.dma_start(big[:, e * 2048:(e + 1) * 2048].rearrange("p (k n) -> p k n", k=DK),
                              io["L0_ffn_w1"][e].rearrange("(k p) n -> p k n", p=P)).then_inc(experts_loaded, 16)
            for e in range(8):
                if e == 7:
                    after_L0a(eng)
                at = 16384 + e * 2048
                eng.dma_start(big[:, at:at + 2048].rearrange("p (k n) -> p k n", k=8),
                              io["L0_ffn_w2"][e].rearrange("(k p) n -> p k n", p=P)).then_inc(experts_loaded, 16)

        xw_flat = xw[:].rearrange("p i k n -> p (i k n)")
        f_qkv, f_out = (t.rearrange("p (k n) -> p k n", k=DK) for t in carve(xw_flat, [DK * 3 * D, DK * D]))
        after = add(norm_tokens("L0f_norm1", x, tokA, after_L0a))
        after = add(norm_tokens("L0f_norm2", tokA, tokB, after))
        L0f = self_attention(
            "L0f", tokB, tokA, [(w_rows("L0_ffn_w_qkv"), f_qkv), (w_rows("L0_ffn_w_proj"), f_out)],
            f_qkv, f_out, after, ln=("L0f_ln1_w", "L0f_ln1_b"), bias=False, load_after=after_L0x)
        layers.append(dict(sp=L0f[0].pop("sp")))
        early = len(layers)
        layers.append(dict(sp=load_experts))
        layers.append(L0f[0])
        after_L0f = L0f[1]
        after = add(norm_tokens("L0f_norm3", tokA, tokB, after_L0f))
        before_experts = len(layers)
        after = add(experts_top1("L0m", tokA, tokB, (row("L0f_ln2_w"), row("L0f_ln2_b")),
                                 w_rows("L0_ffn_gate_w"), row("L0f_gate_b"), after))
        after_L0m = after

        def load_rows(eng):
            after_L0m(eng)
            eng.dma_start(rows[:, 0:NROWS1], io["rows1"].broadcast_to([P, NROWS1])).then_inc(setup_loaded, 16)

        narrow, s_qkv, s_out = (t.rearrange("p (k n) -> p k n", k=DK) for t in
                                carve(saw, [DK * 384, DK * 3 * D, DK * D]))
        L1x, after_L1x = cross_attention("L1x", [io["L1_xattn_" + w] for w in ("Wq", "Wk", "Wv", "Wo")], after_L0m,
                                         after_L0f)
        L1a_norm, after = norm_tokens("L1a_norm", x, tokA, after_L1x)
        L1a, after_L1a = wide_attention("L1a", tokA, io["L1_attn_rel_emb"], after, after_L0m, after_L1x)
        layers.insert(before_experts, dict(sp=L1x.pop("sp_weights")))
        layers += [dict(sp=load_rows), L1x, L1a_norm, L1a]

        x_kept = sem("x_kept")
        x_turned = sem("x_turned")

        def turn_x(eng):
            for c in range(TILES):
                after_L1a(eng, c + 1)
                eng.dma_start(io["scratch_x"][c * P:(c + 1) * P], x[:, c]).then_inc(x_kept, 16)
            eng.wait_ge(x_kept, 16 * TILES)
            turned = io["scratch_x"].rearrange("(i c j) n -> j i c n", j=SPT, c=TILES)
            for j in range(SPT):
                eng.dma_start(x[j * SEQ:(j + 1) * SEQ], turned[j]).then_inc(x_turned, 16)

        def after_turn(eng):
            eng.wait_ge(x_turned, 16 * SPT)

        layers.append(dict(sp=turn_x))
        after = add(norm_tokens("L1f_norm1", x, tokA, after_turn))
        after = add(norm_tokens("L1f_norm2", tokA, tokB, after))
        L1f, after = self_attention(
            "L1f", tokB, tokA, [(w_rows("L1_ffn_qkv_weightT"), narrow), (w_rows("L1_ffn_proj_weightT"), s_out)],
            s_qkv, s_out, after, mask="mask_L1f", ln=("L1f_ln1_w", "L1f_ln1_b"), bias=False,
            spread_kv=(narrow, D), load_after=after_L0a)
        layers.insert(early + 1, dict(sp=L1f.pop("sp")))
        layers.append(L1f)
        after = add(norm_tokens("L1f_norm3", tokA, tokB, after))
        L1m, after = experts_top2("L1m", tokA, tokB, (row("L1f_ln2_w"), row("L1f_ln2_b")),
                                  w_rows("L1_ffn_router_weightT"), after, after_L1a)
        layers.insert(len(layers) - 4, dict(sp=L1m.pop("sp_weights")))
        layers.append(L1m)
        block = ctx.enter_context(nc.Block())

        @block.sync
        def _(sync):
            sync.dma_start(x[:], io["x"].rearrange("(c p) d -> p c d", p=P)).then_inc(x_loaded, 16)
            sync.dma_start(consts[:], io["consts"]).then_inc(setup_loaded, 16)
            sync.dma_start(cols[:], io["cols"]).then_inc(setup_loaded, 16)
            sync.dma_start(rows[:], io["rows0"].broadcast_to([P, NROWS])).then_inc(setup_loaded, 16)
            for layer in layers:
                if "sp" in layer:
                    layer["sp"](sync)
            after(sync)
            turned = out.rearrange("(i c j) n -> j i c n", j=SPT, c=TILES)
            for j in range(SPT):
                sync.dma_start(turned[j], x[j * SEQ:(j + 1) * SEQ]).then_inc(out_stored, 16)
            sync.wait_ge(out_stored, 16 * SPT)

        @block.gpsimd
        def _(pool):
            pool.memset(minus_half[:], -0.5).then_inc(constants_set, 1)
            pool.memset(zeros[:], 0.0).then_inc(zeros_set, 1)
            for layer in layers:
                if "pool" in layer:
                    layer["pool"](pool)

        @block.tensor
        def _(pe):
            for layer in layers:
                if "pe" in layer:
                    layer["pe"](pe)

        @block.scalar
        def _(act):
            for layer in layers:
                if "act" in layer:
                    layer["act"](act)

        @block.vector
        def _(dve):
            for layer in layers:
                if "dve" in layer:
                    layer["dve"](dve)


def _shape_constants():
    import numpy as np
    p = np.arange(P)
    first, second = p % SEQ, p // SEQ
    earlier = first[:, None] < first[None]
    table = {
        "ident": np.eye(P),
        "qmask": (p[:, None] // HD) % HPG == np.arange(HPG)[None],
        "scaled_qmask": ((p[:, None] // HD) % HPG == np.arange(HPG)[None]) * HD ** -0.5,
        "vmask": p[:, None] // SEQ == np.arange(HPG)[None],
        "fold": p[:, None] % SEQ == np.arange(SEQ)[None],
        "own_batch": np.broadcast_to((np.arange(SEQS)[:, None] % 8 == np.arange(8)[None]).reshape(1, -1),
                                     (P, SEQS * 8)),
        "group_mask": p[:, None] % GROUPS == np.arange(GROUPS)[None],
        "same_head": p[:, None] // HD == p[None] // HD,
        "not_first": np.broadcast_to(p[None] % SEQ != 0, (P, P)),
        "row_not_first": p[:, None] % SEQ != 0,
        "mask_L0a": np.where(np.arange(SEQ)[None] < p[:, None] % SEQ, 0.0, MASKED),
        "before": p[:, None] < p[None],
        "ones": np.ones((P, P)),
        "countdown": np.broadcast_to(16 - np.arange(16), (P, 16)),
        "multiples": np.broadcast_to(P * np.arange(TILES), (P, TILES)),
        "upto": np.broadcast_to((np.arange(8)[:, None] >= np.arange(8)[None]).reshape(1, -1), (P, 64)),
        "iota": np.broadcast_to(np.arange(16), (P, 16)),
        "before_own": earlier | ((first[:, None] == first[None]) & (second[:, None] < second[None])),
        "before_lower": first[:, None] <= first[None],
        "before_upper": earlier,
        "first_slot": np.broadcast_to(160 * np.arange(16), (P, 16)),
        "mask_L1f": np.where(np.arange(SEQ)[None] <= p[:, None] % SEQ, 0.0, MASKED),
    }
    return np.concatenate([table[n].astype(np.float32) for n in CONSTS], axis=1)


def _bucket_table():
    import numpy as np
    n = np.arange(SEQ)[None, :] - np.arange(SEQ)[:, None]
    bucket = np.where(n < 0, 16, 0)
    n = np.abs(n)
    far = 8 + (np.log(np.maximum(n, 1).astype(np.float32) / 8) / np.log(16.0) * 8 + 1e-4).astype(np.int32)
    bucket = bucket + np.where(n < 8, n, np.minimum(far, 15))
    onehot = np.arange(32)[:, None, None] == bucket[None]
    return np.tile(onehot[:, :, None, :], (1, 1, SPT, 1)).reshape(32, SEQ * P).astype(np.float32)


def kernel(**inputs):
    import numpy as np
    import concourse.bacc as bacc
    from concourse.bass_utils import run_bass_kernel_spmd as run

    a = {k: np.asarray(v) for k, v in inputs.items()}

    def feat_cols(v):
        return v.reshape(DK, P).T

    def half_cols(lo, hi):
        return np.concatenate([lo, hi])[:, None]

    heads_col = lambda v: np.tile(v.reshape(-1), P // HD)[:, None]
    qkv_b, rkv_b, rq_b = a["L0_attn_qkv_b"], a["L0_attn_rkv_b"], a["L0_attn_rq_b"]
    col_of = {
        "L0x_bq": feat_cols(a["L0_xattn_bq"]), "L0x_bk": feat_cols(a["L0_xattn_bk"]),
        "L0x_bv": feat_cols(a["L0_xattn_bv"]), "L1x_bq": feat_cols(a["L1_xattn_bq"]),
        "L1x_bk": feat_cols(a["L1_xattn_bk"]), "L1x_bv": feat_cols(a["L1_xattn_bv"]),
        "L0a_bk": feat_cols(qkv_b[D:2 * D]), "L0a_bv": feat_cols(qkv_b[2 * D:]),
        "L0a_rout_b": feat_cols(a["L0_attn_rout_b"]),
        "L0a_rkq_b": half_cols(rkv_b[:64], rq_b),
        "L0a_rv_b": half_cols(rkv_b[64:], rkv_b[64:]),
        "L0a_gl": heads_col(a["L0_attn_gl_w"]), "L0a_gr": heads_col(a["L0_attn_gr_w"]),
        "L0f_ln1_w": feat_cols(a["L0_ffn_ln1_w"]), "L0f_ln1_b": feat_cols(a["L0_ffn_ln1_b"]),
        "L1f_ln1_w": feat_cols(a["L1_ffn_ln1_weight"]), "L1f_ln1_b": feat_cols(a["L1_ffn_ln1_bias"]),
    }
    row_of = {
        "L0x_bo": a["L0_xattn_bo"], "L0a_bo": a["L0_attn_out_b"], "L0f_ln2_w": a["L0_ffn_ln2_w"],
        "L0f_ln2_b": a["L0_ffn_ln2_b"], "L1x_bo": a["L1_xattn_bo"], "L1a_bo": a["L1_attn_bo"],
        "L1f_ln2_w": a["L1_ffn_ln2_weight"], "L1f_ln2_b": a["L1_ffn_ln2_bias"], "L0f_gate_b": a["L0_ffn_gate_b"],
        "L0a_bq": qkv_b[:D], "L0a_rq_b": rq_b,
    }
    ctx = a["ctx_1024"]
    arrays = {
        "x": a["x"].reshape(TOK, D),
        "ctxT": ctx.reshape(SEQS, CTX, DK, P).transpose(0, 3, 2, 1),
        "ctx_lastT": ctx[:, CTX - 1].T,
        "cols": np.concatenate([col_of[n] for n in COLS], axis=1),
        "rows0": np.concatenate([row_of[n] for n in ROWS if n[:2] == "L0"])[None],
        "rows1": np.concatenate([row_of[n] for n in ROWS if n[:2] == "L1"])[None],
        "consts": _shape_constants(),
    }
    for n in ("Wq", "Wk", "Wv", "Wo"):
        arrays["L0_xattn_" + n] = a["L0_xattn_" + n]
    for n in ("qkv_w", "out_w", "rq_w", "rkv_w", "rout_w"):
        arrays["L0_attn_" + n] = a["L0_attn_" + n]
    nc = bacc.Bacc("TRN2", target_bir_lowering=False, num_devices=1)
    for n in ("w_qkv", "w_proj", "gate_w", "w1", "w2"):
        arrays["L0_ffn_" + n] = a["L0_ffn_" + n]
    for n in ("Wq", "Wk", "Wv", "Wo"):
        arrays["L1_xattn_" + n] = a["L1_xattn_" + n].T
    for n in ("Wq", "Wkv", "Wo", "rel_emb"):
        arrays["L1_attn_" + n] = a["L1_attn_" + n]
    for n in ("qkv_weight", "proj_weight", "router_weight"):
        arrays["L1_ffn_" + n + "T"] = a["L1_ffn_" + n].T
    for n in ("w1", "w2"):
        arrays["L1_ffn_" + n + "T"] = a["L1_ffn_moe_" + n].transpose(0, 2, 1)
    arrays["buckets"] = _bucket_table()
    arrays = {k: np.ascontiguousarray(v) for k, v in arrays.items()}
    io = {k: nc.dram_tensor("in_" + k, v.shape, mybir.dt.from_np(v.dtype), kind="ExternalInput").ap()
          for k, v in arrays.items()}
    out = nc.dram_tensor("out", (TOK, D), F32, kind="ExternalOutput").ap()
    for name, n in (("scratch_in0", 15 * P), ("scratch_out0", 15 * P), ("scratch_in1", 20 * P),
                    ("scratch_out1", 20 * P), ("scratch_x", TOK)):
        io[name] = nc.dram_tensor(name, (n, D), F32, kind="Internal").ap()
    kernel_program(nc, io, out)
    r = run(nc, [{"in_" + k: v for k, v in arrays.items()}], core_ids=[0])
    return r.results[0]["out"].reshape(SEQS, SEQ, D)
```
